# Optimizing a Trainium2 kernel written in Bass

```python
import numpy as np
import jax
import jax.numpy as jnp

def _softmax(x, axis=-1):
    return jax.nn.softmax(x, axis=axis)

def _gelu(x):
    return jax.nn.gelu(x, approximate=True)

def _silu(x):
    return jax.nn.silu(x)

def _sigmoid(x):
    return jax.nn.sigmoid(x)

def _layernorm(x, axis=-1, eps=1e-05):
    m = jnp.mean(x, axis=axis, keepdims=True)
    v = jnp.var(x, axis=axis, keepdims=True)
    return (x - m) / jnp.sqrt(v + eps)

def _scatter_add(tgt, idx, src, axis=0):
    return tgt.at[idx].add(src)

def _segment_sum(src, seg, n):
    return jax.ops.segment_sum(src, seg, n)
kernel_name = 'mk_adj_seq_d1_adj_r2_9e42ae'

def setup_inputs(seed: int=0):
    np.random.seed(seed)
    _w = jnp.asarray

    def _rec_inputs():
        import jax
        import jax.numpy as jnp
        _gk = jax.random.key(seed)
        x = -0.003407 + 1.001 * jax.random.normal(jax.random.fold_in(_gk, 1), (2048, 128), jnp.float32)
        _a = jax.random.bernoulli(jax.random.fold_in(_gk, 2), 0.00195312, (2048, 2048))
        adj = _a.astype(jnp.int32)
        return (x, adj)
    x, adj = _rec_inputs()

    def _L0_gnn_setup():
        import jax, jax.numpy as jnp
        import numpy as np
        LAYER_IDX = 2
        T = 5
        K = 2
        EXP_DILATION = False
        QUANTILES = (0.25, 0.5, 0.75)
        SELF_RATIO = 0.5
        USE_SELF = True
        RESIDUAL = True
        key = jax.random.key(seed)
        kx, ka, kw = jax.random.split(key, 3)
        N, D = (512, 128)
        x = jax.random.normal(kx, (N, D), dtype=jnp.float32)
        A = (jax.random.uniform(ka, (N, N)) < 0.05).astype(jnp.int32)
        W = jax.random.normal(kw, (D, D), dtype=jnp.float32) / np.sqrt(D).astype(np.float32)
        b = jnp.zeros((D,), dtype=jnp.float32)
        return {'x': x, 'A': A, 'W': W, 'b': b}
    _L0_gnn_all = _L0_gnn_setup()
    _L0_gnn_in = {k: v for k, v in _L0_gnn_all.items() if k in ('W', 'b')}
    del _L0_gnn_all
    return {'x': x, 'adj': adj, 'L0_gnn_W': _L0_gnn_in['W'], 'L0_gnn_b': _L0_gnn_in['b']}

def reference(x, adj, L0_gnn_W, L0_gnn_b):
    import jax
    import jax.numpy as jnp

    def _L0_gnn_ref(x, A, W, b):
        import jax, jax.numpy as jnp
        import numpy as np
        LAYER_IDX = 2
        T = 5
        K = 2
        EXP_DILATION = False
        QUANTILES = (0.25, 0.5, 0.75)
        SELF_RATIO = 0.5
        USE_SELF = True
        RESIDUAL = True
        N, D = x.shape
        mask = A != 0
        rank = jnp.cumsum(mask.astype(jnp.int32), axis=1) - 1
        num_nbr = mask.sum(axis=1)
        m_i = jnp.where(num_nbr > T, jnp.ceil(num_nbr / K).astype(jnp.int32), jnp.int32(1))
        skip = m_i * (2 ** (LAYER_IDX - 1) if EXP_DILATION else 1)
        remove = mask & ((rank + 1) % skip[:, None] == 0)
        keep = mask & ~remove
        n_keep = keep.sum(axis=1)
        big = jnp.finfo(x.dtype).max
        vals = jnp.where(keep[:, :, None], x[None, :, :], big)
        svals = jnp.sort(vals, axis=1)
        w_q = jnp.asarray(1.0 / len(QUANTILES), x.dtype)
        agg = jnp.zeros((N, D), x.dtype)
        for q in QUANTILES:
            idx = jnp.maximum(jnp.ceil(q * n_keep).astype(jnp.int32) - 1, 0)
            picked = jnp.take_along_axis(svals, idx[:, None, None], axis=1)[:, 0, :]
            agg = agg + w_q * picked
        agg = jnp.where((n_keep > 0)[:, None], agg, jnp.zeros((), x.dtype))
        if USE_SELF:
            agg = (1.0 - SELF_RATIO) * agg + SELF_RATIO * x
        out = agg @ W.T + b
        if RESIDUAL:
            out = out + x
        return out
    x = _L0_gnn_ref(x, adj, L0_gnn_W, L0_gnn_b)
    return x

_drawn_inputs = setup_inputs


def setup_inputs(seed=0):
    import zlib

    import numpy as np

    out = dict(_drawn_inputs(seed))
    spreads = {'L0_gnn_b': (0.0, 0.1)}
    factors = {}
    for name, (base, spread) in spreads.items():
        noise = np.random.default_rng([zlib.crc32(name.encode()), seed]).standard_normal(out[name].shape)
        drawn = base * np.exp(spread * noise) if base else spread * noise
        out[name] = jnp.asarray(drawn.astype(out[name].dtype))
    for name, factor in factors.items():
        out[name] = (out[name] * factor).astype(out[name].dtype)
    return out
```

```python
from contextlib import ExitStack

import numpy as np
import concourse.bass as bass
from concourse import mybir

F32 = mybir.dt.float32
F16 = mybir.dt.float16
I32 = mybir.dt.int32
U32 = mybir.dt.uint32
ALU = mybir.AluOpType
ACT = mybir.ActivationFunctionType
AX = mybir.AxisListType

P = 128
N = 2048
D = 128
NT = N // P
BITS = 4
GROUPS = N // BITS
QUARTERS = 4
GQ = GROUPS // QUARTERS
WORDS = 8 * QUARTERS
BIG = float(np.finfo(np.float32).max)
THIRD = float(np.float32(1.0 / 3.0))
MAGIC = float(3 << 22)

LCAP = 64
MB, SB = 2, 2
NB = 1 + MB + SB
NS = NB * P
CAPS = (SB * P, MB * P, LCAP)
OFFS = ((1 + MB) * P, P, 0)
FIELDS = 2 * WORDS + 3
M_RANKS = (0, 1, 2, 4, 5, 6)
S_RANKS = (0, 1, 3, 4)
LH = 7
G_M = LH
G_S = G_M + MB * len(M_RANKS)
G_X = G_S + SB * len(S_RANKS)
NG = G_X + NB
FINISH = ((0,), tuple(range(1 + MB, NB)), tuple(range(1, 1 + MB)))
MASKS = 4
RING = 8

H_DIAG, H_ID, H_TRI, H_ONES, H_GRP, H_SLOT, H_TP = np.cumsum([0, 4 * P, P, P, P, GROUPS, NS])
H_END = int(H_TP) + 2 * NT
C_ID, C_CAP, C_OFF, C_LO, C_HI, C_V = np.cumsum([0, P, 3 * NT, 3 * NT, 4, 4])
C_END = int(C_V) + LH


def constants():
    h = np.zeros((P, H_END), np.float16)
    eye = np.eye(P)
    for b in range(BITS):
        h[:, H_DIAG + b * P:H_DIAG + (b + 1) * P] = eye * (GROUPS << b)
    h[:, H_ID:H_TRI] = eye
    h[:, H_TRI:H_ONES] = np.triu(np.ones((P, P)), 1)
    h[:, H_ONES:H_GRP] = 1
    h[:, H_GRP:H_SLOT] = GROUPS - 1 - np.arange(GROUPS)
    slots = np.arange(NS) + 1
    slots[LCAP:P] -= LCAP
    h[:, H_SLOT:H_TP] = slots
    tp = np.zeros((P, NT, 2))
    tp[:, :, 0] = np.arange(NT)
    tp[:, :, 1] = np.arange(P)[:, None]
    h[:, H_TP:] = tp.reshape(P, -1)
    c = np.zeros((P, C_END), np.float32)
    c[:, C_ID:C_CAP] = eye
    c[:, C_CAP:C_OFF] = np.repeat(CAPS, NT)
    c[:, C_OFF:C_LO] = np.repeat(np.array(OFFS) + 1, NT)
    c[:, C_LO:C_HI] = (9, 11, 13, 15)
    c[:, C_HI:C_V] = (10, 12, 14, 16)
    c[:, C_V:] = 2 * np.arange(LH) + 3
    return h, c


def build(nc, x, adj, w, b, hconst, cconst, out):
    ctx = ExitStack()
    with ctx:
        def sb(name, shape, dt):
            return ctx.enter_context(nc.sbuf_tensor(name, shape, dt))

        def pb(name, shape, dt):
            return ctx.enter_context(nc.psum_tensor(name, shape, dt))

        def sem(name):
            return ctx.enter_context(nc.semaphore(name))

        A = sb("A", [P, RING, N], I32)
        mask = sb("mask", [P, MASKS, N], F16)
        hc = sb("hc", [P, H_END], F16)
        cc = sb("cc", [P, C_END], F32)
        xs = sb("xs", [P, 4, D], F32)
        xT = sb("xT", [P, N], F32)
        base = sb("base", [P, 4, 4, D], F32)
        wsb = sb("wsb", [P, D], F32)
        wT = sb("wT", [P, D], F32)
        wTi = sb("wTi", [P, D], F32)
        brow = sb("brow", [1, D], F32)
        onerow = sb("onerow", [1, P], F32)
        codes = sb("codes", [P, NT, WORDS], I32)
        part = sb("part", [P, NT, 2, WORDS], I32)
        rec = sb("rec", [P, NT, FIELDS], F16)
        junk = sb("junk", [P, 2, N], F16)
        cnt = sb("cnt", [P, NT], F32)
        full = sb("full", [P, NT], F32)
        ok = sb("ok", [P, NT], F32)
        le8 = sb("le8", [P, NT], F32)
        le16 = sb("le16", [P, NT], F32)
        cls = sb("cls", [P, 3, NT], F16)
        fits = sb("fits", [P, 3, NT], F32)
        at = sb("at", [P, 3, NT], F32)
        slot = sb("slot", [P, NT], F32)
        placed = sb("placed", [P, NT], F32)
        fb = sb("fb", [P, NT], F16)
        fbn = sb("fbn", [P, 1], I32)
        fbnf = sb("fbnf", [P, 1], F32)
        fbpos = sb("fbpos", [P, NT], F32)
        fbat = sb("fbat", [P, NT], I32)
        fbrow = sb("fbrow", [P, NT], I32)
        fm = sb("fm", [P, 2], F32)
        fk = sb("fk", [P, 3], F32)
        fcnt = sb("fcnt", [P, 3], F32)
        fpre = sb("fpre", [P, 3], I32)
        fbit = sb("fbit", [P, 3], I32)
        fcand = sb("fcand", [P, 3], I32)
        fsgn = sb("fsgn", [P, 3], I32)
        fval = sb("fval", [P, 3], I32)
        ftake = sb("ftake", [P, 3], I32)
        fcol = sb("fcol", [P, 1], F32)
        fxcol = sb("fxcol", [P, 1], F32)
        frow = sb("frow", [1, D], F32)
        rowlist = nc.dram_tensor("rowlist", (N, 1), I32, kind="Internal").ap()
        hot = sb("hot", [P, 2, NS], F16)
        R = sb("R", [P, NB, FIELDS], F32)
        rid = sb("rid", [P, NB], F32)
        rown = sb("rown", [P, NB], I32)
        K = sb("K", [P, NB, WORDS], I32)
        grp = sb("grp", [P, NB, WORDS], I32)
        bit = sb("bit", [P, BITS, NB, WORDS], I32)
        keys = sb("keys", [P, NB, BITS, WORDS], F32)
        keyr = sb("keyr", [P, BITS * WORDS], F32)
        top = sb("top", [P, NB + 1, 8], F32)
        eq = sb("eq", [P, 4], F32)
        em = sb("em", [P, 4], F32)
        lv = sb("lv", [P, LH], F32)
        lk = sb("lk", [P, 4, LH], F32)
        nbL = sb("nbL", [P, LH], I32)
        nb = sb("nb", [P, MB + SB, 8], I32)
        G = sb("G", [P, NG, D], F32)
        Lraw = sb("Lraw", [P, LH, P], F32)
        scr = sb("scr", [P, 13, P], F32)
        Ls = sb("Ls", [P, LH, 2, LCAP], F32)
        s8 = sb("s8", [P, 8, LCAP], F32)
        s8b = sb("s8b", [P, 8, LCAP], F32)
        u6 = sb("u6", [P, 6, LCAP], F32)
        u4 = sb("u4", [P, 6, LCAP], F32)
        r810 = sb("r810", [P, 2, LCAP], F32)
        tri3 = sb("tri3", [P, 4, LCAP], F32)
        diagw = sb("diagw", [LCAP, 4, LCAP], F16)
        S2 = sb("S2", [P, 12, MB, D], F32)
        T3 = sb("T3", [P, 4, MB, D], F32)
        slotempty = sb("slotempty", [P, NB], F32)
        agg = sb("agg", [P, MB + SB, D], F32)
        aggT = sb("aggT", [P, NS], F32)
        gxT = sb("gxT", [P, NB, P], F32)
        y = sb("y", [P, NB, D], F32)

        ps_code = pb("ps_code", [P, 2, GROUPS], F32)
        ps_misc = pb("ps_misc", [P, 512], F32)
        ps_rec = pb("ps_rec", [P, 512], F32)
        ps_t = pb("ps_t", [P, 2, 512], F32)
        ps_o = pb("ps_o", [P, 2, 512], F32)
        before = ps_misc[:, 0:3 * NT].rearrange("p (c t) -> p c t", c=3)
        lweight = ps_misc[:, 256:512].rearrange("p (h r) -> p h r", h=4)
        fbcount = ps_misc[:, 64:64 + NT]
        fbfront = ps_misc[:, 96:96 + NT]
        fout = ps_misc[0:1, 128:128 + D]
        finish = [ps_rec, ps_o[:, 1, :], ps_o[:, 0, :]]
        recs = ps_rec[:, 0:NB * FIELDS].rearrange("p (k f) -> p k f", k=NB)

        s_adj = [sem(f"s_adj{t}") for t in range(NT)]
        s_h = sem("s_h")
        s_c = sem("s_c")
        s_w = sem("s_w")
        s_b = sem("s_b")
        s_x = [sem(f"s_x{g}") for g in range(4)]
        s_mask = sem("s_mask")
        s_code = sem("s_code")
        s_word = sem("s_word")
        s_cnt = sem("s_cnt")
        s_v = sem("s_v")
        s_part = sem("s_part")
        s_rec = sem("s_rec")
        s_cls = sem("s_cls")
        s_bef = sem("s_bef")
        s_hot = sem("s_hot")
        s_put = sem("s_put")
        s_R = sem("s_R")
        s_row = sem("s_row")
        s_nb = sem("s_nb")
        s_nbL = sem("s_nbL")
        s_fill = sem("s_fill")
        s_g = [sem(f"s_g{g}") for g in range(NG)]
        s_dw = sem("s_dw")
        s_lw = sem("s_lw")
        s_lt = sem("s_lt")
        s_lraw = sem("s_lraw")
        s_aggL = sem("s_aggL")
        s_agg = sem("s_agg")
        s_xt = sem("s_xt")
        s_xc = sem("s_xc")
        s_at = sem("s_at")
        s_ac = sem("s_ac")
        s_y = sem("s_y")
        s_yc = sem("s_yc")
        s_wt = sem("s_wt")
        s_wc = sem("s_wc")
        s_wti = sem("s_wti")
        s_bt = sem("s_bt")
        s_btc = sem("s_btc")
        s_bo = sem("s_bo")
        s_bc = sem("s_bc")
        s_bst = sem("s_bst")
        s_sc = sem("s_sc")
        s_one = sem("s_one")
        s_fb = sem("s_fb")
        s_fbc = sem("s_fbc")
        s_fbn = sem("s_fbn")
        s_fpre = sem("s_fpre")
        s_fat = sem("s_fat")
        s_list = sem("s_list")
        s_fa = sem("s_fa")
        s_fc = sem("s_fc")
        s_fp = sem("s_fp")
        s_fy = sem("s_fy")
        s_fo = sem("s_fo")
        s_fs = sem("s_fs")

        block = ctx.enter_context(nc.Block())
        x_t = x.rearrange("(g k p) d -> g p k d", k=4, p=P)
        out_t = out.rearrange("(g k p) d -> g p k d", k=4, p=P)

        @block.sync
        def _(sp):
            def adjacency(t):
                if t >= RING:
                    sp.wait_ge(s_mask, t - RING + 1)
                sp.dma_start(A[:, t % RING, :], adj[t * P:(t + 1) * P, :]).then_inc(s_adj[t], 16)

            adjacency(0)
            sp.dma_start(hc[:], hconst).then_inc(s_h, 16)
            adjacency(1)
            sp.dma_start(cc[:], cconst).then_inc(s_c, 16)
            sp.dma_start(wsb[:], w).then_inc(s_w, 16)
            sp.dma_start(brow[:], b).then_inc(s_b, 16)
            for t in range(2, NT):
                if t % 3 == 2 and t // 3 < 4:
                    g = t // 3
                    if g >= 1:
                        sp.wait_ge(s_bt, g)
                    sp.dma_start(xs[:], x_t[g]).then_inc(s_x[g], 16)
                adjacency(t)
            for g in range(4):
                sp.wait_ge(s_bc, g + 1)
                sp.dma_start(out_t[g], base[:, g]).then_inc(s_bst, 16)
            sp.wait_ge(s_bst, 64)

            sp.wait_ge(s_fbn, 1)
            sp.wait_ge(s_sc, 16 * NB)
            n = sp.value_load(fbn[0:1, 0:1], min_val=0, max_val=N)
            with sp.If(n > 0):
                sp.wait_ge(s_mask, NT)
                sp.wait_ge(s_list, 16 * NT)
                with sp.Fori(0, n) as i:
                    row = sp.value_load(rowlist[bass.ds(i, 1), :], min_val=0, max_val=N - 1)
                    sp.dma_start(A[:, 0, :], adj[bass.ds(row, 1), :].to_broadcast([P, N])).then_inc(s_fa, 16)
                    sp.wait_ge(s_fy, i + 1)
                    sp.dma_start(out[bass.ds(row, 1), :], frow[:]).then_inc(s_fo, 16)
                    sp.wait_ge(s_fo, i * 16 + 16)
                    sp.sem_inc(s_fs, 1)

        @block.gpsimd
        def _(pool):
            nc.gpsimd.memset(G[:, 0:G_M, :], BIG).then_inc(s_fill, 1)
            nc.gpsimd.memset(G[:, G_M:NG, :], 0.0).then_inc(s_fill, 1)
            pool.wait_ge(s_fill, 2)

            def gather(g, index):
                nc.gpsimd.indirect_dma_start(
                    G[:, g, :], None, x[:, :], bass.IndirectOffsetOnAxis(ap=index.bitcast(U32), axis=0),
                    bounds_check=N - 1, oob_is_err=False).then_inc(s_g[g], 16)

            pool.wait_ge(s_nbL, 1)
            for j in range(LH):
                gather(j, nbL[:, j:j + 1])
            pool.wait_ge(s_nb, 1)
            for k in range(MB):
                for j, r in enumerate(M_RANKS):
                    gather(G_M + k * len(M_RANKS) + j, nb[:, k, r:r + 1])
            for k in range(SB):
                for j, r in enumerate(S_RANKS):
                    gather(G_S + k * len(S_RANKS) + j, nb[:, MB + k, r:r + 1])
            pool.wait_ge(s_row, 1)
            for k in range(NB):
                gather(G_X + k, rown[:, k:k + 1])
            pool.wait_ge(s_bst, 64)
            for k in (k for blocks in FINISH for k in blocks):
                pool.wait_ge(s_yc, 1 + [k in blocks for blocks in FINISH].index(True))
                rows = LCAP if k == 0 else P
                nc.gpsimd.indirect_dma_start(
                    out[:, :], bass.IndirectOffsetOnAxis(ap=rown[0:rows, k:k + 1].bitcast(U32), axis=0),
                    y[0:rows, k, :], None, bounds_check=N - 1, oob_is_err=False).then_inc(s_sc, 16)
            pool.wait_ge(s_sc, 16 * NB)

            pool.wait_ge(s_fbn, 1)
            n = pool.value_load(fbn[0:1, 0:1], min_val=0, max_val=N)
            with pool.If(n > 0):
                pool.wait_ge(s_fat, 1)
                for t in range(NT):
                    nc.gpsimd.indirect_dma_start(
                        rowlist[:, :], bass.IndirectOffsetOnAxis(ap=fbat[:, t:t + 1].bitcast(U32), axis=0),
                        fbrow[:, t:t + 1], None, bounds_check=N - 1, oob_is_err=False).then_inc(s_list, 16)

        @block.scalar
        def _(act):
            copy = nc.scalar.copy
            act.wait_ge(s_wt, 1)
            copy(wT[:], ps_t[:, 0, 0:D]).then_inc(s_wc, 1)
            for t in range(NT):
                act.wait_ge(s_mask, t + 1)
                if t >= 2:
                    act.wait_ge(s_cnt, t - 1)
                nc.scalar.activation(junk[:, t % 2, :], mask[:, t % MASKS, :], ACT.Copy,
                                     accum_out=cnt[:, t:t + 1]).then_inc(s_cnt, 1)
                if t % 3 == 0 and 3 <= t < 15:
                    g = t // 3 - 1
                    act.wait_ge(s_bt, g + 1)
                    copy(xT[:, g * 512:(g + 1) * 512], ps_t[:, g % 2, :]).then_inc(s_btc, 1)
                    act.wait_ge(s_bo, g + 1)
                    copy(base[:, g].rearrange("p k d -> p (k d)"), ps_o[:, g % 2, :]).then_inc(s_bc, 1)
            act.wait_ge(s_part, 1)
            copy(rec[:, :, 0:2 * WORDS], part[:].rearrange("p t a w -> p t (a w)"))
            copy(rec[:, :, 2 * WORDS:2 * WORDS + 2], hc[:, H_TP:H_END].rearrange("p (t a) -> p t a", a=2))
            act.wait_ge(s_cnt, NT)
            copy(rec[:, :, 2 * WORDS + 2], cnt[:]).then_inc(s_rec, 1)
            act.wait_ge(s_put, NT)
            copy(R[:], recs).then_inc(s_R, 1)
            for c in range(2):
                act.wait_ge(s_lt, c + 1)
                k = (4, 3)[c]
                nc.scalar.activation(Lraw[:, 4 * c:4 * c + k, :].rearrange("p j q -> p (j q)"),
                                     ps_t[:, c, 0:k * P], ACT.Copy, scale=THIRD / 2).then_inc(s_lraw, 1)
            act.wait_ge(s_xt, 1)
            copy(gxT[:, 0:4, :].rearrange("p k q -> p (k q)"), ps_o[:, 0, :]).then_inc(s_xc, 1)
            act.wait_ge(s_xt, 2)
            copy(gxT[:, 4, :], ps_o[:, 1, 0:P]).then_inc(s_xc, 1)
            act.wait_ge(s_at, 1)
            nc.scalar.activation(aggT[:, P:NS], ps_t[:, 0, 0:NS - P], ACT.Copy,
                                 scale=THIRD / 2).then_inc(s_ac, 1)
            for part_of, blocks in enumerate(FINISH):
                act.wait_ge(s_y, part_of + 1)
                rows = LCAP if 0 in blocks else P
                copy(y[0:rows, blocks[0]:blocks[-1] + 1, :].rearrange("p k d -> p (k d)"),
                     finish[part_of][0:rows, 0:len(blocks) * D]).then_inc(s_yc, 1)

        @block.tensor
        def _(pe):
            ident = cc[:, C_ID:C_ID + P]
            pe.wait_ge(s_c, 16)
            pe.wait_ge(s_w, 16)
            pe.transpose(ps_t[:, 0, 0:D], wsb[:], ident).then_inc(s_wt, 1)
            pe.wait_ge(s_h, 16)
            for t in range(NT):
                pe.wait_ge(s_mask, t + 1)
                if t >= 2:
                    pe.wait_ge(s_word, t - 1)
                for q in range(BITS):
                    pe.matmul(ps_code[:, t % 2, :], hc[:, H_DIAG + q * P:H_DIAG + (q + 1) * P],
                              mask[:, t % MASKS, q * GROUPS:(q + 1) * GROUPS], start=(q == 0), stop=False)
                pe.matmul(ps_code[:, t % 2, :], hc[:, H_ID:H_ID + P], hc[:, H_GRP:H_GRP + GROUPS],
                          start=False, stop=True).then_inc(s_code, 1)
                if t % 3 == 2 and t // 3 < 4:
                    g = t // 3
                    pe.wait_ge(s_x[g], 16)
                    if g == 0:
                        pe.wait_ge(s_wc, 1)
                    if g >= 2:
                        pe.wait_ge(s_btc, g - 1)
                    for k in range(4):
                        last = pe.transpose(ps_t[:, g % 2, k * P:(k + 1) * P], xs[:, k, :], ident)
                    last.then_inc(s_bt, 1)
                    if g == 0:
                        pe.wait_ge(s_wti, 1)
                        pe.wait_ge(s_b, 16)
                        pe.wait_ge(s_one, 1)
                if t % 3 == 0 and 3 <= t < 15:
                    g = t // 3 - 1
                    pe.wait_ge(s_btc, g + 1)
                    if g >= 2:
                        pe.wait_ge(s_bc, g - 1)
                    for k in range(4):
                        o = ps_o[:, g % 2, k * D:(k + 1) * D]
                        pe.matmul(o, xT[:, (4 * g + k) * P:(4 * g + k + 1) * P], wTi[:], start=True, stop=False)
                        last = pe.matmul(o, onerow[:], brow[:], start=False, stop=True)
                    last.then_inc(s_bo, 1)

            pe.wait_ge(s_cls, 1)
            pe.matmul(before, hc[:, H_TRI:H_TRI + P], cls[:], start=True, stop=False)
            for t in range(NT - 1):
                last = pe.matmul(before[:, :, t + 1:NT], hc[:, H_ONES:H_ONES + P],
                                 cls[:, :, t:t + 1].to_broadcast([P, 3, NT - 1 - t]),
                                 start=False, stop=(t == NT - 2))
            last.then_inc(s_bef, 1)
            pe.wait_ge(s_rec, 1)
            for t in range(NT):
                pe.wait_ge(s_hot, t + 1)
                for k in range(NB):
                    last = pe.matmul(recs[:, k, :], hot[:, t % 2, k * P:(k + 1) * P], rec[:, t, :],
                                     start=(t == 0 and k == 0), stop=(t == NT - 1), skip_group_check=True)
                last.then_inc(s_put, 1)
            pe.wait_ge(s_fb, 1)
            pe.matmul(fbcount, hc[:, H_ONES:H_ONES + P], fb[:], start=True, stop=True).then_inc(s_fbc, 1)
            pe.wait_ge(s_fbn, 1)
            pe.wait_ge(s_dw, 1)
            pe.matmul(lweight, hc[0:LCAP, H_ONES:H_ONES + P], diagw[:], start=True, stop=True).then_inc(s_lw, 1)
            for j in range(LH):
                pe.wait_ge(s_g[j], 16)
                last = pe.transpose(ps_t[:, j // 4, (j % 4) * P:(j % 4 + 1) * P], G[:, j, :], ident)
                if j in (3, LH - 1):
                    last.then_inc(s_lt, 1)
            for k in range(NB):
                pe.wait_ge(s_g[G_X + k], 16)
                last = pe.transpose(ps_o[:, k // 4, (k % 4) * P:(k % 4 + 1) * P], G[:, G_X + k, :], ident)
                if k in (3, NB - 1):
                    last.then_inc(s_xt, 1)
            pe.wait_ge(s_lraw, 1)
            for k in range(MB + SB):
                pe.wait_ge(s_agg, 1 if k >= MB else 2)
                last = pe.transpose(ps_t[:, 0, k * P:(k + 1) * P], agg[:, k, :], ident)
            last.then_inc(s_at, 1)
            pe.wait_ge(s_xc, 2)
            for part_of, blocks in enumerate(FINISH):
                pe.wait_ge(*((s_aggL, 1) if 0 in blocks else (s_ac, 1)))
                for j, k in enumerate(blocks):
                    rows = LCAP if k == 0 else P
                    o = finish[part_of][0:rows, j * D:(j + 1) * D]
                    pe.matmul(o, aggT[:, k * P:k * P + rows], wT[:], start=True, stop=False)
                    pe.matmul(o, gxT[:, k, 0:rows], wTi[:], start=False, stop=False)
                    last = pe.matmul(o, onerow[:, 0:rows], brow[:], start=False, stop=True)
                last.then_inc(s_y, 1)

            n = pe.value_load(fbn[0:1, 0:1], min_val=0, max_val=N)
            with pe.If(n > 0):
                pe.matmul(fbfront, hc[:, H_TRI:H_TRI + P], fb[:], start=True, stop=False)
                for t in range(NT - 1):
                    last = pe.matmul(fbfront[:, t + 1:NT], hc[:, H_ONES:H_ONES + P],
                                     fb[:, t:t + 1].to_broadcast([P, NT - 1 - t]), start=False, stop=(t == NT - 2))
                last.then_inc(s_fpre, 1)
                with pe.Fori(0, n) as i:
                    pe.wait_ge(s_fc, i + 1)
                    pe.matmul(fout, fcol[:], wT[:], start=True, stop=False)
                    pe.matmul(fout, fxcol[:], wTi[:], start=False, stop=False)
                    pe.matmul(fout, onerow[:, 0:1], brow[:], start=False, stop=True).then_inc(s_fp, 1)

        @block.vector
        def _(dve):
            V = nc.vector
            steps = [0]

            def step(instruction):
                steps[0] += 1
                return instruction.then_inc(s_v, 1)

            def settle():
                dve.wait_ge(s_v, steps[0])

            def network(layers, start, pool, final):
                place, free = dict(start), list(pool)
                uses = {}
                for n, layer in enumerate(layers):
                    for a, b in layer:
                        uses[a] = uses[b] = n
                for n, layer in enumerate(layers):
                    used = []
                    for a, b in layer:
                        ins = place[a], place[b]
                        for e, op in ((a, ALU.min), (b, ALU.max)):
                            if uses[e] == n and final.get(e) is None:
                                place[e] = None
                                continue
                            o = final[e] if uses[e] == n else free.pop(0)
                            step(V.tensor_tensor(o, ins[0], ins[1], op))
                            place[e] = o
                        used += ins
                    free += [u for u in used if any(u is f for f in pool)]
                    settle()

            V.memset(onerow[:], 1.0).then_inc(s_one, 1)

            def make_mask(t):
                dve.wait_ge(s_adj[t], 16)
                if t >= MASKS:
                    dve.wait_ge(s_code, t - MASKS + 1)
                    dve.wait_ge(s_cnt, t - MASKS + 1)
                V.tensor_scalar(mask[:, t % MASKS, :], A[:, t % RING, :], 0.0, None, ALU.not_equal).then_inc(s_mask, 1)

            make_mask(0)
            dve.wait_ge(s_wc, 1)
            V.scalar_tensor_tensor(wTi[:], wT[:], 0.5, cc[:, C_ID:C_ID + P], ALU.mult, ALU.add).then_inc(s_wti, 1)
            make_mask(1)
            for t in range(NT):
                if t + 2 < NT:
                    make_mask(t + 2)
                dve.wait_ge(s_code, t + 1)
                for q in range(QUARTERS):
                    last = V.max(codes[:, t, 8 * q:8 * q + 8], ps_code[:, t % 2, q * GQ:(q + 1) * GQ])
                last.then_inc(s_word, 1)

            dve.wait_ge(s_word, NT)
            V.tensor_single_scalar(part[:, :, 0, :], codes[:], 127, ALU.bitwise_and)
            V.tensor_single_scalar(part[:, :, 1, :], codes[:], 7, ALU.logical_shift_right).then_inc(s_part, 1)
            step(V.tensor_reduce(full[:], codes[:].rearrange("p t (q e) -> p t q e", e=8)[:, :, :, 7], AX.X, ALU.max))
            settle()
            step(V.tensor_scalar(ok[:], full[:], float(GROUPS), None, ALU.is_lt))
            settle()
            dve.wait_ge(s_cnt, NT)
            step(V.scalar_tensor_tensor(cls[:, 0], cnt[:], 6.0, ok[:], ALU.is_equal, ALU.mult))
            step(V.scalar_tensor_tensor(le8[:], cnt[:], 8.0, ok[:], ALU.is_le, ALU.mult))
            step(V.scalar_tensor_tensor(le16[:], cnt[:], 16.0, ok[:], ALU.is_le, ALU.mult))
            settle()
            step(V.scalar_tensor_tensor(cls[:, 1], cnt[:], 7.0, le8[:], ALU.is_ge, ALU.mult))
            step(V.scalar_tensor_tensor(cls[:, 2], cnt[:], 9.0, le16[:], ALU.is_ge, ALU.mult))
            settle()
            V.tensor_copy(le8[:], le16[:]).then_inc(s_cls, 1)
            capt = cc[:, C_CAP:C_OFF].rearrange("p (c t) -> p c t", c=3)
            offt = cc[:, C_OFF:C_LO].rearrange("p (c t) -> p c t", c=3)
            dve.wait_ge(s_bef, 1)
            step(V.tensor_tensor(fits[:], before, capt, ALU.is_lt))
            step(V.tensor_tensor(at[:], before, offt, ALU.add))
            settle()
            step(V.tensor_tensor(fits[:], fits[:], cls[:], ALU.mult))
            settle()
            step(V.tensor_tensor(at[:], at[:], fits[:], ALU.mult))
            settle()
            step(V.tensor_reduce(slot[:], at[:].rearrange("p c t -> p t c"), AX.X, ALU.add))
            step(V.tensor_reduce(placed[:], fits[:].rearrange("p c t -> p t c"), AX.X, ALU.add))
            settle()
            for t in range(NT):
                if t >= 2:
                    dve.wait_ge(s_put, t - 1)
                V.tensor_scalar(hot[:, t % 2, :], hc[:, H_SLOT:H_TP], slot[:, t:t + 1], None,
                                ALU.is_equal).then_inc(s_hot, 1)
            V.scalar_tensor_tensor(fb[:], cnt[:], 6.0, placed[:], ALU.is_ge, ALU.subtract).then_inc(s_fb, 1)

            dve.wait_ge(s_R, 1)
            step(V.scalar_tensor_tensor(K[:], R[:, :, WORDS:2 * WORDS], 128.0, R[:, :, 0:WORDS], ALU.mult, ALU.add))
            step(V.scalar_tensor_tensor(rid[:], R[:, :, 2 * WORDS], float(P), R[:, :, 2 * WORDS + 1], ALU.mult, ALU.add))
            n_of = R[:, :, 2 * WORDS + 2]
            step(V.tensor_scalar(slotempty[:], n_of, 0.0, float(2 * N), ALU.is_equal, ALU.mult))
            settle()
            V.tensor_tensor(rown[:], rid[:], slotempty[:], ALU.add).then_inc(s_row, 1)
            step(V.tensor_single_scalar(grp[:], K[:], GROUPS - 1, ALU.bitwise_and))
            for q in range(BITS):
                step(V.tensor_scalar(bit[:, q], K[:], 9 + q, 1, ALU.logical_shift_right, ALU.bitwise_and))
            settle()
            for q in range(BITS):
                step(V.scalar_tensor_tensor(keys[:, :, q, :], grp[:], float(1 + GROUPS * (BITS - 1 - q)), bit[:, q],
                                            ALU.add, ALU.mult))
            settle()
            flat = keys[:].rearrange("p k b w -> p k (b w)")
            step(V.max(top[:, 0, :], flat[:, 0, :]))
            settle()
            step(V.match_replace(keyr[:], top[:, 0, :], flat[:, 0, :], 0.0))
            settle()
            step(V.max(top[:, 1, :], keyr[:]))
            nL = R[:, 0, 2 * WORDS + 2:2 * WORDS + 3]
            step(V.tensor_scalar(eq[:], cc[:, C_LO:C_LO + 4], nL, None, ALU.is_equal))
            step(V.tensor_scalar(lv[:], cc[:, C_V:C_V + LH], nL, None, ALU.is_le))
            settle()
            step(V.scalar_tensor_tensor(em[:], cc[:, C_HI:C_HI + 4], nL, eq[:], ALU.is_equal, ALU.add))
            settle()
            tl = top[:, 0:2, :].rearrange("p a b -> p (a b)")
            h = LCAP
            step(V.tensor_copy(lk[0:h, 3, :], tl[0:h, 0:LH]))
            step(V.tensor_scalar(lk[h:P, 0, :], tl[h:P, 5:5 + LH], em[h:P, 0:1], None, ALU.mult))
            for i in range(1, 4):
                settle()
                step(V.scalar_tensor_tensor(lk[h:P, i, :], tl[h:P, 5 + i:5 + i + LH], em[h:P, i:i + 1], lk[h:P, i - 1, :],
                                            ALU.mult, ALU.add))
            settle()
            step(V.tensor_tensor(lk[:, 0, :], lk[:, 3, :], lv[:], ALU.mult))
            settle()
            V.tensor_scalar(nbL[:], lk[:, 0, :], -1.0, float(N), ALU.mult, ALU.add).then_inc(s_nbL, 1)
            dve.wait_ge(s_fbc, 1)
            step(V.tensor_reduce(fbnf[:], fbcount, AX.X, ALU.add))
            settle()
            V.tensor_copy(fbn[:], fbnf[:]).then_inc(s_fbn, 1)
            for k in range(1, NB):
                step(V.max(top[:, 1 + k, :], flat[:, k, :]))
            settle()
            V.tensor_scalar(nb[:], top[:, 2:, :], -1.0, float(N), ALU.mult, ALU.add).then_inc(s_nb, 1)
            for i in range(4):
                last = V.tensor_scalar(diagw[:, i, :], hc[0:LCAP, H_ID:H_ID + LCAP], em[0:LCAP, i:i + 1], None, ALU.mult)
            last.then_inc(s_dw, 1)

            dve.wait_ge(s_lraw, 2)
            network([[(0, 6), (2, 3), (4, 5)], [(0, 2), (1, 4), (3, 6)], [(0, 1), (2, 5), (3, 4)],
                     [(1, 2), (4, 6)], [(2, 3), (4, 5)], [(1, 2), (3, 4), (5, 6)]],
                    {i: Lraw[:, i, :] for i in range(LH)}, [scr[:, i, :] for i in range(13)],
                    {i: Ls[:, i].rearrange("p s r -> p (s r)") for i in range(LH)})
            low, high = Ls[:, :, 0, :], Ls[:, :, 1, :]
            step(V.tensor_copy(s8[:, 0, :], low[:, 0, :]))
            step(V.tensor_copy(s8[:, 7, :], high[:, 0, :]))
            for i in range(1, LH):
                step(V.tensor_tensor(s8[:, i, :], low[:, i, :], high[:, LH - i, :], ALU.min))
                step(V.tensor_tensor(u6[:, i - 1, :], low[:, i, :], high[:, LH - i, :], ALU.max))
            settle()
            step(V.tensor_tensor(s8b[:, 0:4, :], s8[:, 0:4, :], s8[:, 4:8, :], ALU.min))
            step(V.tensor_tensor(s8b[:, 4:8, :], s8[:, 0:4, :], s8[:, 4:8, :], ALU.max))
            step(V.tensor_tensor(u4[:, 0, :], u6[:, 0, :], u6[:, 4, :], ALU.min))
            step(V.tensor_tensor(u4[:, 1, :], u6[:, 1, :], u6[:, 5, :], ALU.min))
            settle()
            b2 = lambda v: v[:].rearrange("p (a b c) r -> p a b (c r)", a=2, b=2)
            step(V.tensor_tensor(b2(s8)[:, :, 0], b2(s8b)[:, :, 0], b2(s8b)[:, :, 1], ALU.min))
            step(V.tensor_tensor(b2(s8)[:, :, 1], b2(s8b)[:, :, 0], b2(s8b)[:, :, 1], ALU.max))
            step(V.tensor_tensor(u4[:, 2, :], u6[:, 3, :], u4[:, 1, :], ALU.min))
            step(V.tensor_tensor(u4[:, 3, :], u6[:, 3, :], u4[:, 1, :], ALU.max))
            step(V.tensor_tensor(u4[:, 4, :], u6[:, 2, :], u4[:, 0, :], ALU.min))
            step(V.tensor_tensor(u4[:, 5, :], u6[:, 2, :], u4[:, 0, :], ALU.max))
            settle()
            b1 = lambda v: v[:].rearrange("p (a b) r -> p a b r", b=2)
            step(V.tensor_tensor(b1(s8b)[:, :, 0], b1(s8)[:, :, 0], b1(s8)[:, :, 1], ALU.min))
            step(V.tensor_tensor(b1(s8b)[:, :, 1], b1(s8)[:, :, 0], b1(s8)[:, :, 1], ALU.max))
            step(V.tensor_tensor(r810[:, 0, :], u4[:, 2, :], u4[:, 4, :], ALU.min))
            step(V.tensor_tensor(r810[:, 1, :], u4[:, 3, :], u4[:, 5, :], ALU.min))
            settle()
            rank = {**{i: s8b[:, i, :] for i in range(8)}, 8: r810[:, 0, :], 10: r810[:, 1, :]}
            picks = [(1, 3, 5), (2, 4, 7), (2, 5, 8), (3, 6, 10)]
            for i, (r0, r1, r2) in enumerate(picks):
                step(V.tensor_tensor(tri3[:, i, :], rank[r0], rank[r1], ALU.add))
            settle()
            for i, (r0, r1, r2) in enumerate(picks):
                step(V.tensor_tensor(s8[:, i, :], tri3[:, i, :], rank[r2], ALU.add))
            settle()
            dve.wait_ge(s_lw, 1)
            step(V.tensor_tensor(tri3[:], lweight, s8[:, 0:4, :], ALU.mult))
            settle()
            V.tensor_reduce(aggT[:, 0:LCAP], tri3[:].rearrange("p h r -> p r h"), AX.X, ALU.add).then_inc(s_aggL, 1)

            for g in range(G_S, G_X):
                dve.wait_ge(s_g[g], 16)
            gs = G[:, G_S:G_X, :].rearrange("p (k j) d -> p j k d", k=SB)
            sv = lambda i: S2[:, i]
            step(V.tensor_tensor(sv(0), gs[:, 0], gs[:, 1], ALU.min))
            step(V.tensor_tensor(sv(1), gs[:, 0], gs[:, 1], ALU.max))
            step(V.tensor_tensor(sv(2), gs[:, 2], gs[:, 3], ALU.min))
            step(V.tensor_tensor(sv(3), gs[:, 2], gs[:, 3], ALU.max))
            settle()
            step(V.tensor_tensor(sv(4), sv(1), sv(3), ALU.min))
            step(V.tensor_tensor(sv(5), sv(0), sv(2), ALU.add))
            settle()
            V.tensor_tensor(agg[:, MB:MB + SB], sv(4), sv(5), ALU.add).then_inc(s_agg, 1)

            gm = G[:, G_M:G_S, :].rearrange("p (k j) d -> p j k d", k=MB)
            for g in range(G_M, G_S):
                dve.wait_ge(s_g[g], 16)
            dve.wait_ge(s_agg, 1)
            fin = {1: T3[:, 0], 2: T3[:, 1], 4: T3[:, 2]}
            network([[(0, 5), (1, 3), (2, 4)], [(1, 2), (3, 4)], [(0, 3), (2, 5)], [(0, 1), (2, 3), (4, 5)],
                     [(1, 2), (3, 4)]],
                    {i: gm[:, i] for i in range(6)}, [S2[:, i] for i in range(12)], fin)
            step(V.tensor_tensor(T3[:, 3], T3[:, 0], T3[:, 1], ALU.add))
            settle()
            V.tensor_tensor(agg[:, 0:MB], T3[:, 3], T3[:, 2], ALU.add).then_inc(s_agg, 1)

            dve.wait_ge(s_fbn, 1)
            n = dve.value_load(fbn[0:1, 0:1], min_val=0, max_val=N)
            with dve.If(n > 0):
                is_nb, rnk = A[:, 1, :].bitcast(F32), A[:, 2, :].bitcast(F32)
                kept, vals, below = A[:, 3, :], A[:, 4, :].bitcast(F32), A[:, 5, :].bitcast(F32)
                ones = A[:, 6, :].bitcast(F32)
                V.memset(ones, 1.0)
                tp = hc[:, H_TP:H_END].rearrange("p (t a) -> p t a", a=2)
                dve.wait_ge(s_fpre, 1)
                V.tensor_scalar(fbpos[:], fb[:], -2.0 * N, 2.0 * N, ALU.mult, ALU.add)
                dve.drain()
                V.tensor_tensor(fbat[:], fbpos[:], fbfront, ALU.add)
                V.scalar_tensor_tensor(fbrow[:], tp[:, :, 0], float(P), tp[:, :, 1], ALU.mult, ALU.add).then_inc(s_fat, 1)
                dve.wait_ge(s_list, 16 * NT)
                with dve.Fori(0, n) as i:
                    row = dve.value_load(rowlist[bass.ds(i, 1), :], min_val=0, max_val=N - 1)
                    V.tensor_copy(fxcol[:], xT[:, bass.ds(row, 1)])
                    V.memset(vals, BIG)
                    V.memset(fpre[:], 0)
                    V.memset(fbit[:], -2**31)
                    dve.wait_ge(s_fa, i * 16 + 16)
                    V.tensor_scalar(is_nb, A[:, 0, :], 0.0, None, ALU.not_equal)
                    dve.drain()
                    V.tensor_tensor_scan(rnk, ones, is_nb, 0.0, ALU.mult, ALU.add)
                    dve.drain()
                    V.tensor_scalar(fm[:, 1:2], rnk[:, N - 1:N], 0.5, 0.25, ALU.mult, ALU.add)
                    dve.drain()
                    V.tensor_scalar(fm[:, 0:1], fm[:, 1:2], MAGIC, -MAGIC, ALU.add, ALU.add)
                    dve.drain()
                    V.tensor_scalar(fm[:, 1:2], fm[:, 0:1], 2.0, None, ALU.mult)
                    V.scalar_tensor_tensor(is_nb, rnk, fm[:, 0:1], is_nb, ALU.not_equal, ALU.mult)
                    for j, q in enumerate((0.25, 0.5, 0.75)):
                        V.tensor_scalar(fk[:, j:j + 1], fm[:, 0:1], 2 * q, 0.375 - 2 * q, ALU.mult, ALU.add)
                    dve.drain()
                    V.scalar_tensor_tensor(kept, rnk, fm[:, 1:2], is_nb, ALU.not_equal, ALU.mult)
                    V.tensor_scalar(fcnt[:], fk[:], MAGIC, -MAGIC, ALU.add, ALU.add)
                    dve.drain()
                    V.copy_predicated(vals, kept, xT[:])
                    V.tensor_scalar(fk[:], fcnt[:], -1.0, None, ALU.add)
                    dve.drain()
                    with dve.Fori(0, 32):
                        V.tensor_tensor(fcand[:], fpre[:], fbit[:], ALU.bitwise_or)
                        dve.drain()
                        V.tensor_scalar(fsgn[:], fcand[:], 31, -1, ALU.arith_shift_right, ALU.bitwise_xor)
                        dve.drain()
                        V.scalar_tensor_tensor(fval[:], fsgn[:], -2**31, fcand[:], ALU.bitwise_or, ALU.bitwise_xor)
                        dve.drain()
                        for j in range(3):
                            V.tensor_scalar(below, vals, fval[:, j:j + 1].bitcast(F32), None, ALU.is_lt, ALU.add,
                                            accum_out=fcnt[:, j:j + 1])
                            dve.drain()
                        V.tensor_tensor(ftake[:], fcnt[:], fk[:], ALU.is_le)
                        dve.drain()
                        V.copy_predicated(fpre[:], ftake[:], fcand[:])
                        dve.drain()
                        V.tensor_single_scalar(fbit[:], fbit[:], 1, ALU.logical_shift_right)
                        dve.drain()
                    V.tensor_scalar(fsgn[:], fpre[:], 31, -1, ALU.arith_shift_right, ALU.bitwise_xor)
                    dve.drain()
                    V.scalar_tensor_tensor(fval[:], fsgn[:], -2**31, fpre[:], ALU.bitwise_or, ALU.bitwise_xor)
                    dve.drain()
                    V.tensor_scalar(fcnt[:], fval[:].bitcast(F32), THIRD / 2, None, ALU.mult)
                    dve.drain()
                    V.tensor_reduce(fcol[:], fcnt[:], AX.X, ALU.add).then_inc(s_fc, 1)
                    dve.wait_ge(s_fp, i + 1)
                    V.tensor_copy(frow[:], fout).then_inc(s_fy, 1)


def kernel(x, adj, L0_gnn_W, L0_gnn_b):
    import concourse.bacc as bacc
    from concourse.bass_utils import run_bass_kernel_spmd as run

    nc = bacc.Bacc("TRN2", target_bir_lowering=False, num_devices=1)
    hconst, cconst = constants()
    arrays = {
        "x_dram": np.ascontiguousarray(x),
        "adj_dram": np.ascontiguousarray(adj),
        "w_dram": np.ascontiguousarray(L0_gnn_W),
        "b_dram": np.ascontiguousarray(L0_gnn_b).reshape(1, D),
        "hconst_dram": hconst,
        "cconst_dram": cconst,
    }
    args = [nc.dram_tensor(k, a.shape, mybir.dt.from_np(a.dtype), kind="ExternalInput").ap()
            for k, a in arrays.items()]
    out = nc.dram_tensor("out_dram", (N, D), F32, kind="ExternalOutput").ap()
    build(nc, *args, out)
    return run(nc, [arrays], core_ids=[0]).results[0]["out_dram"]
```

```python
from contextlib import ExitStack

import numpy as np
import concourse.bass as bass
from concourse import mybir

F32 = mybir.dt.float32
F16 = mybir.dt.float16
BF16 = mybir.dt.bfloat16
I32 = mybir.dt.int32
U32 = mybir.dt.uint32
ALU = mybir.AluOpType
ACT = mybir.ActivationFunctionType
AX = mybir.AxisListType

P = 128
N = 2048
D = 128
NT = N // P
BITS = 4
GROUPS = N // BITS
QUARTERS = 4
GQ = GROUPS // QUARTERS
WORDS = 8 * QUARTERS
BIG = float(np.finfo(np.float32).max)
THIRD = float(np.float32(1.0 / 3.0))
MAGIC = float(3 << 22)

S, M, L, X = range(4)
LEAST, MOST = (6, 7, 9, 13), (6, 8, 12, 16)
M_RANKS = (0, 1, 2, 4, 5, 6)
S_RANKS = (0, 1, 3, 4)
MR, SR = len(M_RANKS), len(S_RANKS)
SIDE = 7


class Phase:

    def __init__(self, lo, hi, xcap):
        self.lo, self.hi, self.tiles = lo, hi, hi - lo
        self.caps = (P, P, LUSED - xcap, xcap)
        self.lcap = LUSED - xcap


LSLOTS = P // 2
LUSED = 40
BLOCKS = 3
G_M, G_S = SIDE, SIDE + MR
NG = SIDE + MR + SR
PHASES = (Phase(0, NT // 2, 4), Phase(NT // 2, NT, 4))
OFFS = lambda ph: (2 * P, P, 0, ph.lcap)
ACT_TILES = (8, 10, 12, 14)
FIELDS = 2 * WORDS + 3
LEAD = 1
MASKS = 4
RING = 8

H_DIAG, H_ID, H_TRI, H_ONES, H_GRP, H_TP, H_SLOT = np.cumsum([0, 4 * P, P, P, P, GROUPS, 2 * NT]).tolist()
H_END = H_SLOT + BLOCKS * P
C_ID, C_LEAST, C_MOST, C_LO, C_HI, C_V, C_CAP = np.cumsum([0, P, 4, 4, 4, 4, SIDE + 1]).tolist()
C_END = C_CAP + 16


def constants():
    h = np.zeros((P, H_END), np.float16)
    eye = np.eye(P)
    for b in range(BITS):
        h[:, H_DIAG + b * P:H_DIAG + (b + 1) * P] = eye * (GROUPS << b)
    h[:, H_ID:H_TRI] = eye
    h[:, H_TRI:H_ONES] = np.triu(np.ones((P, P)), 1)
    h[:, H_ONES:H_GRP] = 1
    h[:, H_GRP:H_TP] = GROUPS - 1 - np.arange(GROUPS)
    tp = np.zeros((P, NT, 2))
    tp[:, :, 0] = np.arange(NT)
    tp[:, :, 1] = np.arange(P)[:, None]
    h[:, H_TP:H_SLOT] = tp.reshape(P, -1)
    slots = np.arange(BLOCKS * P) + 1
    slots[:P] = np.arange(P) % LSLOTS + 1
    h[:, H_SLOT:H_END] = slots
    c = np.zeros((P, C_END), np.float32)
    c[:, C_ID:C_LEAST] = eye
    c[:, C_LEAST:C_MOST] = LEAST
    c[:, C_MOST:C_LO] = MOST
    c[:, C_LO:C_HI] = (9, 11, 13, 15)
    c[:, C_HI:C_V] = (10, 12, 14, 16)
    c[:, C_V:C_CAP] = 2 * np.arange(SIDE + 1) + 3
    for f, ph in enumerate(PHASES):
        c[:, C_CAP + 8 * f:C_CAP + 8 * f + 4] = ph.caps
        c[:, C_CAP + 8 * f + 4:C_CAP + 8 * f + 8] = np.array(OFFS(ph)) + 1
    return h, c


def build(nc, x, adj, w, b, hconst, cconst, out):
    ctx = ExitStack()
    with ctx:
        def sb(name, shape, dt):
            return ctx.enter_context(nc.sbuf_tensor(name, shape, dt))

        def pb(name, shape, dt):
            return ctx.enter_context(nc.psum_tensor(name, shape, dt))

        def sem(name):
            return ctx.enter_context(nc.semaphore(name))

        A = sb("A", [P, RING, N], I32)
        mask = sb("mask", [P, MASKS, N], F16)
        junk = sb("junk", [P, 2, N], F16)
        hc = sb("hc", [P, H_END], F16)
        cc = sb("cc", [P, C_END], F32)
        xs = sb("xs", [P, NT, D], F32)
        xT = sb("xT", [P, N], F32)
        base = sb("base", [P, NT, D], F32)
        wsb = sb("wsb", [P, D], F32)
        wT = sb("wT", [P, D], F32)
        wTi = sb("wTi", [P, D], F32)
        brow = sb("brow", [1, D], F32)
        b4 = sb("b4", [1, 4, D], F32)
        bleft = sb("bleft", [1, 2, 4, D], F32)
        bparts = sb("bparts", [1, 3, 4, D], BF16)
        oneb = sb("oneb", [1, P], BF16)
        onerow = sb("onerow", [1, P], F32)
        codes = sb("codes", [P, NT, WORDS], I32)
        part = sb("part", [P, NT, 2, WORDS], I32)
        rec = sb("rec", [P, NT, FIELDS], F16)
        cnt = sb("cnt", [P, NT], F32)
        full = sb("full", [P, NT], F32)
        ok = sb("ok", [P, NT], F32)
        placed = sb("placed", [P, NT], F32)
        slot = sb("slot", [P, NT], F32)
        fb = sb("fb", [P, NT], F16)

        hot = sb("hot", [P, max(ph.tiles for ph in PHASES), BLOCKS * P], F16)

        class Bufs:

            def __init__(self, f, ph):
                def own(name, shape, dt):
                    return sb(f"{name}{f}", shape, dt)

                nb = BLOCKS
                self.ge = own("ge", [P, 4, ph.tiles], F32)
                self.le = own("le", [P, 4, ph.tiles], F32)
                self.cls = own("cls", [P, 4, ph.tiles], F16)
                self.fits = own("fits", [P, 4, ph.tiles], F32)
                self.at = own("at", [P, 4, ph.tiles], F32)
                self.R = own("R", [P, nb, FIELDS], F32)
                self.rid = own("rid", [P, nb], F32)
                self.none = own("none", [P, nb], F32)
                self.bits = own("bits", [P, nb, WORDS], I32)
                self.bit = own("bit", [P, BITS, nb, WORDS], I32)
                self.keys = own("keys", [P, nb, BITS, WORDS], F32)
                self.keyr = own("keyr", [P, BITS * WORDS], F32)
                self.top = own("top", [P, nb + 1, 8], F32)
                self.eq = own("eq", [P, 4], F32)
                self.em = own("em", [P, 4], F32)
                self.lv = own("lv", [P, 8], F32)
                self.lk = own("lk", [P, 4, 8], F32)
                self.lkv = own("lkv", [P, 8], F32)
                self.nbL = own("nbL", [P, 8], I32)
                self.nb = own("nb", [P, nb - 1, 8], I32)
                self.G = own("G", [P, NG, D], F32)
                self.diagw = own("diagw", [LSLOTS, 4, LUSED], F16)
                self.Lraw = own("Lraw", [P, SIDE, 2, LUSED], F32)
                self.small = own("small", [P, LUSED, 8], F32)
                xcap = LUSED - ph.lcap
                self.xpos = own("xpos", [P, 2 * SIDE, xcap], F32)
                self.large = own("large", [P, xcap, 8], F32)
                self.sums = own("sums", [P, 2, LUSED], F32)
                self.sumt = own("sumt", [P, 2, LUSED], F32)
                self.agg = own("agg", [P, 2, D], F32)
                self.s_part = sem(f"s_part{f}")
                self.s_rec = sem(f"s_rec{f}")
                self.s_cls = sem(f"s_cls{f}")
                self.s_bef = sem(f"s_bef{f}")
                self.s_hot = sem(f"s_hot{f}")
                self.s_put = sem(f"s_put{f}")
                self.s_R = sem(f"s_R{f}")
                self.s_nbL = sem(f"s_nbL{f}")
                self.s_nb = sem(f"s_nb{f}")
                self.s_fill = sem(f"s_fill{f}")
                self.s_g = [sem(f"s_g{f}_{g}") for g in range(NG)]
                self.s_em = sem(f"s_em{f}")
                self.s_dw = sem(f"s_dw{f}")
                self.s_lw = sem(f"s_lw{f}")
                self.s_lt = sem(f"s_lt{f}")
                self.s_lraw = sem(f"s_lraw{f}")
                self.s_agg = [sem(f"s_agg{f}_{k}") for k in range(2)]
                self.s_aggL = sem(f"s_aggL{f}")

        B = [Bufs(f, ph) for f, ph in enumerate(PHASES)]
        scr = sb("scr", [P, 12, D], F32)
        s4 = sb("s4", [P, 6, D], F32)
        ENDS = ((0, 1), (0, 2), (1, 1), (None, 0), (1, 2))
        ends = range(len(ENDS))
        LX = ENDS.index((None, 0))
        aggT = sb("aggT", [P, len(ENDS), P], F32)
        endrow = sb("endrow", [P, len(ENDS)], I32)
        own = sb("own", [P, len(ENDS), D], F32)
        ownT = sb("ownT", [P, len(ENDS), P], F32)
        y = sb("y", [P, len(ENDS), D], F32)
        fbn = sb("fbn", [P, 1], I32)
        fbnf = sb("fbnf", [P, 1], F32)
        fbj = sb("fbj", [P, NT], F32)
        fbpos = sb("fbpos", [P, NT], F32)
        fbat = sb("fbat", [P, NT], I32)
        fbrow = sb("fbrow", [P, NT], I32)
        fm = sb("fm", [P, 2], F32)
        fk = sb("fk", [P, 3], F32)
        fcnt = sb("fcnt", [P, 3], F32)
        fpre = sb("fpre", [P, 3], I32)
        fbit = sb("fbit", [P, 3], I32)
        fcand = sb("fcand", [P, 3], I32)
        fsgn = sb("fsgn", [P, 3], I32)
        fval = sb("fval", [P, 3], I32)
        ftake = sb("ftake", [P, 3], I32)
        fcol = sb("fcol", [P, 1], F32)
        fxcol = sb("fxcol", [P, 1], F32)
        frow = sb("frow", [1, D], F32)
        rowlist = nc.dram_tensor("rowlist", (N, 1), I32, kind="Internal").ap()
        ps_code = pb("ps_code", [P, 2, GROUPS], F32)
        ps_misc = pb("ps_misc", [P, 512], F32)
        ps_rec = pb("ps_rec", [P, 512], F32)
        ps_t = pb("ps_t", [P, 2, 512], F32)
        ps_o = pb("ps_o", [P, 2, 512], F32)
        fbcount = ps_rec[:, 512 - NT:]
        fbfront = ps_misc[:, 96:96 + NT]
        fout = ps_misc[0:1, 128:128 + D]
        turned = ps_code[:, 1, 0:P]
        finish = [ps_code[:, 0, 0:D], ps_rec[:, 0:D], ps_o[:, 1, 0:D]]

        def before(ph):
            return ps_misc[:, 0:4 * ph.tiles].rearrange("p (c t) -> p c t", c=4)

        def lweight():
            return ps_misc[:, 256:256 + 4 * LUSED].rearrange("p (h r) -> p h r", h=4)

        recs = ps_rec[:, 0:BLOCKS * FIELDS].rearrange("p (k f) -> p k f", k=BLOCKS)

        s_adj = [sem(f"s_adj{t}") for t in range(NT)]
        s_h = sem("s_h")
        s_c = sem("s_c")
        s_w = sem("s_w")
        s_b = sem("s_b")
        s_x = sem("s_x")
        s_mask = sem("s_mask")
        s_amask = sem("s_amask")
        s_sign = sem("s_sign")
        s_bp = sem("s_bp")
        s_endrow = sem("s_endrow")
        s_own = [sem(f"s_own{e}") for e in ends]
        s_at = sem("s_at")
        s_ac = sem("s_ac")
        s_ot = sem("s_ot")
        s_oc = sem("s_oc")
        s_sc = sem("s_sc")
        s_code = sem("s_code")
        s_word = sem("s_word")
        s_cnt = [sem("s_cnt"), sem("s_acnt")]
        s_v = sem("s_v")
        s_wt = sem("s_wt")
        s_wc = sem("s_wc")
        s_wti = sem("s_wti")
        s_bt = sem("s_bt")
        s_btc = sem("s_btc")
        s_bo = sem("s_bo")
        s_bc = sem("s_bc")
        s_bst = sem("s_bst")
        s_y = sem("s_y")
        s_yc = sem("s_yc")
        s_one = sem("s_one")
        s_fill = sem("s_fill")
        s_fb = sem("s_fb")
        s_fbc = sem("s_fbc")
        s_fbf = sem("s_fbf")
        s_fbn = sem("s_fbn")
        s_fpre = sem("s_fpre")
        s_fat = sem("s_fat")
        s_list = sem("s_list")
        s_fa = sem("s_fa")
        s_fc = sem("s_fc")
        s_fp = sem("s_fp")
        s_fy = sem("s_fy")
        s_fo = sem("s_fo")
        s_fs = sem("s_fs")

        def turn_of(e):
            return e + 1 - (e > LX)

        def made(t):
            return sum((i in ACT_TILES) == (t in ACT_TILES) for i in range(t + 1))

        def mask_made(engine, t):
            engine.wait_ge(s_amask if t in ACT_TILES else s_mask, made(t))

        def counted(engine, tiles):
            theirs = sum(t in ACT_TILES for t in range(tiles))
            engine.wait_ge(s_cnt[0], tiles - theirs)
            if theirs:
                engine.wait_ge(s_cnt[1], theirs)

        block = ctx.enter_context(nc.Block())

        @block.sync
        def _(sp):
            for t in range(NT):
                if t >= RING:
                    mask_made(sp, t - RING)
                sp.dma_start(A[:, t % RING, :], adj[t * P:(t + 1) * P, :]).then_inc(s_adj[t], 16)
                if t == 0:
                    sp.dma_start(hc[:], hconst).then_inc(s_h, 16)
                if t == 1:
                    sp.dma_start(cc[:], cconst).then_inc(s_c, 16)
                    sp.dma_start(wsb[:], w).then_inc(s_w, 16)
                    sp.dma_start(brow[:], b).then_inc(s_b, 16)
            sp.dma_start(xs[:], x.rearrange("(k p) d -> p k d", p=P)).then_inc(s_x, 16)
            out_t = out.rearrange("(g k p) d -> g p k d", k=4, p=P)
            for g in range(4):
                sp.wait_ge(s_bc, g + 1)
                sp.dma_start(out_t[g], base[:, 4 * g:4 * g + 4, :]).then_inc(s_bst, 16)
            sp.wait_ge(s_bst, 64)

            sp.wait_ge(s_fbn, 1)
            sp.wait_ge(s_sc, 16 * len(ENDS))
            n = sp.value_load(fbn[0:1, 0:1], min_val=0, max_val=N)
            with sp.If(n > 0):
                mask_made(sp, NT - 1)
                mask_made(sp, ACT_TILES[-1])
                sp.wait_ge(s_list, 16 * NT)
                with sp.Fori(0, n) as i:
                    row = sp.value_load(rowlist[bass.ds(i, 1), :], min_val=0, max_val=N - 1)
                    sp.dma_start(A[:, 0, :], adj[bass.ds(row, 1), :].to_broadcast([P, N])).then_inc(s_fa, 16)
                    sp.wait_ge(s_fy, i + 1)
                    sp.dma_start(out[bass.ds(row, 1), :], frow[:]).then_inc(s_fo, 16)
                    sp.wait_ge(s_fo, i * 16 + 16)
                    sp.sem_inc(s_fs, 1)

        @block.gpsimd
        def _(pool):
            for u in B:
                nc.gpsimd.memset(u.G[:, 0:SIDE, :], BIG).then_inc(u.s_fill, 1)
                nc.gpsimd.memset(u.G[:, SIDE:, :], 0.0).then_inc(u.s_fill, 1)
            nc.gpsimd.memset(own[:], 0.0).then_inc(B[1].s_fill, 1)
            nc.gpsimd.memset(aggT[:, LX, :], 0.0).then_inc(s_fill, 1)

            def gather(to, source, index, done):
                nc.gpsimd.indirect_dma_start(
                    to, None, source[:, :], bass.IndirectOffsetOnAxis(ap=index.bitcast(U32), axis=0),
                    bounds_check=N - 1, oob_is_err=False).then_inc(done, 16)

            def gather_own(e):
                gather(own[:, e, :], x, endrow[:, e:e + 1], s_own[e])

            def gather_lx(u):
                pool.wait_ge(u.s_nbL, 1)
                for j in range(SIDE):
                    gather(u.G[:, j, :], x, u.nbL[:, j:j + 1], u.s_g[j])

            def gather_k(u, k, at, ranks):
                pool.wait_ge(u.s_nb, 1)
                for j, r in enumerate(ranks):
                    gather(u.G[:, at + j, :], x, u.nb[:, k, r:r + 1], u.s_g[at + j])

            pool.wait_ge(B[0].s_fill, 2)
            gather_lx(B[0])
            gather_k(B[0], 0, G_M, M_RANKS)
            gather_k(B[0], 1, G_S, S_RANKS)
            pool.wait_ge(B[1].s_fill, 3)
            gather_k(B[1], 0, G_M, M_RANKS)
            gather_lx(B[1])
            pool.wait_ge(s_endrow, 2)
            for e in ends:
                gather_own(e)
            gather_k(B[1], 1, G_S, S_RANKS)
            pool.wait_ge(s_bst, 64)
            for e in ends:
                pool.wait_ge(s_yc, e + 1)
                nc.gpsimd.indirect_dma_start(
                    out[:, :], bass.IndirectOffsetOnAxis(ap=endrow[:, e:e + 1].bitcast(U32), axis=0),
                    y[:, e, :], None, bounds_check=N - 1, oob_is_err=False).then_inc(s_sc, 16)
            pool.wait_ge(s_sc, 16 * len(ENDS))

            pool.wait_ge(s_fbn, 1)
            n = pool.value_load(fbn[0:1, 0:1], min_val=0, max_val=N)
            with pool.If(n > 0):
                pool.wait_ge(s_fat, 1)
                for t in range(NT):
                    nc.gpsimd.indirect_dma_start(
                        rowlist[:, :], bass.IndirectOffsetOnAxis(ap=fbat[:, t:t + 1].bitcast(U32), axis=0),
                        fbrow[:, t:t + 1], None, bounds_check=N - 1, oob_is_err=False).then_inc(s_list, 16)

        @block.scalar
        def _(act):
            copy = nc.scalar.copy

            def record(f):
                ph, u = PHASES[f], B[f]
                r = slice(ph.lo, ph.hi)
                if f == 0:
                    act.wait_ge(s_h, 16)
                tp = hc[:, H_TP:H_SLOT].rearrange("p (t a) -> p t a", a=2)
                copy(rec[:, r, 2 * WORDS:2 * WORDS + 2], tp[:, r, :])
                counted(act, ph.hi)
                copy(rec[:, r, 2 * WORDS + 2], cnt[:, r])
                act.wait_ge(u.s_part, 1)
                copy(rec[:, r, 0:2 * WORDS], part[:, r].rearrange("p t a w -> p t (a w)")).then_inc(u.s_rec, 1)

            def compacted(f):
                ph, u = PHASES[f], B[f]
                act.wait_ge(u.s_put, ph.tiles)
                copy(u.bits[:], recs[:, :, WORDS:2 * WORDS]).then_inc(u.s_R, 1)
                copy(u.R[:], recs).then_inc(u.s_R, 1)

            def base_rows(g):
                act.wait_ge(s_bt, g + 1)
                copy(xT[:, g * 512:(g + 1) * 512], ps_o[:, 1, :]).then_inc(s_btc, 1)
                act.wait_ge(s_bo, g + 1)
                copy(base[:, 4 * g:4 * g + 4, :].rearrange("p k d -> p (k d)"), ps_o[:, 0, :]).then_inc(s_bc, 1)

            def weights(f):
                u = B[f]
                act.wait_ge(u.s_em, 1)
                for i in range(4):
                    last = nc.scalar.activation(u.diagw[:, i, :], hc[0:LSLOTS, H_ID:H_ID + LUSED], ACT.Copy,
                                                scale=u.em[0:LSLOTS, i:i + 1])
                last.then_inc(u.s_dw, 1)

            def block0(f):
                u = B[f]
                for c, k in enumerate((4, SIDE - 4)):
                    act.wait_ge(u.s_lt, c + 1)
                    sides = ps_t[:, c, 0:k * P].rearrange("p (j c r) -> p (j c) r", c=2, r=LSLOTS)
                    nc.scalar.activation(u.Lraw[:, 4 * c:4 * c + k].rearrange("p j c r -> p (j c) r"),
                                         sides[:, :, 0:LUSED], ACT.Copy, scale=-THIRD / 2)
                    nc.scalar.activation(u.xpos[:, 8 * c:8 * c + 2 * k, :], sides[:, :, PHASES[f].lcap:LUSED],
                                         ACT.Copy, scale=THIRD / 2).then_inc(u.s_lraw, 1)

            def turned_agg(e):
                act.wait_ge(s_at, turn_of(e))
                nc.scalar.activation(aggT[:, e, :], turned, ACT.Copy, scale=THIRD / 2).then_inc(s_ac, 1)

            def make_mask(t):
                act.wait_ge(s_adj[t], 16)
                if t >= MASKS:
                    act.wait_ge(s_code, t - MASKS + 1)
                    act.wait_ge(s_cnt[(t - MASKS) in ACT_TILES], made(t - MASKS))
                m = mask[:, t % MASKS, :]
                n = made(t)
                nc.scalar.activation(m, A[:, t % RING, :], ACT.Sign).then_inc(s_sign, 1)
                act.wait_ge(s_sign, n)
                nc.scalar.activation(m, m, ACT.Square, accum_out=cnt[:, t:t + 1]).then_inc(s_cnt[1], 1)
                act.wait_ge(s_cnt[1], n)
                act.sem_inc(s_amask, 1)

            for t in range(NT):
                if t + LEAD in ACT_TILES:
                    make_mask(t + LEAD)
                if t not in ACT_TILES:
                    mask_made(act, t)
                    n = made(t)
                    if n > 2:
                        act.wait_ge(s_cnt[0], n - 2)
                    nc.scalar.activation(junk[:, n % 2, :], mask[:, t % MASKS, :], ACT.Copy,
                                         accum_out=cnt[:, t:t + 1]).then_inc(s_cnt[0], 1)
                if t == 2:
                    act.wait_ge(s_wt, 1)
                    copy(wT[:], ps_t[:, 0, 0:D]).then_inc(s_wc, 1)
                if t == PHASES[0].hi - 1:
                    record(0)
                if t == PHASES[0].hi + 1:
                    compacted(0)
            record(1)
            compacted(1)
            base_rows(0)
            weights(0)
            block0(0)
            weights(1)
            base_rows(1)
            act.wait_ge(s_fbc, 1)
            nc.scalar.activation(fbj[:], fbcount, ACT.Copy, accum_out=fbnf[:]).then_inc(s_fbf, 1)
            act.wait_ge(s_fbf, 1)
            copy(fbn[:], fbnf[:]).then_inc(s_fbn, 1)
            base_rows(2)
            turned_agg(0)
            turned_agg(1)
            base_rows(3)
            block0(1)
            def turned_own(e):
                act.wait_ge(s_ot, e + 1)
                copy(ownT[:, e, :], ps_o[:, 0, 0:P]).then_inc(s_oc, 1)

            def finished(e):
                act.wait_ge(s_y, e + 1)
                copy(y[:, e, :], finish[e % len(finish)]).then_inc(s_yc, 1)

            for e in (0, 1):
                turned_own(e)
                finished(e)
            turned_agg(2)
            turned_own(2)
            finished(2)
            turned_own(3)
            turned_own(4)
            finished(3)
            turned_agg(4)
            finished(4)

        @block.tensor
        def _(pe):
            ident = cc[:, C_ID:C_ID + P]
            pe.wait_ge(s_h, 16)

            def compact(f):
                ph, u = PHASES[f], B[f]
                pe.wait_ge(u.s_cls, 1)
                pe.matmul(before(ph), hc[:, H_TRI:H_TRI + P], u.cls[:], start=True, stop=False)
                for t in range(ph.tiles - 1):
                    last = pe.matmul(before(ph)[:, :, t + 1:], hc[:, H_ONES:H_ONES + P],
                                     u.cls[:, :, t:t + 1].to_broadcast([P, 4, ph.tiles - 1 - t]),
                                     start=False, stop=(t == ph.tiles - 2))
                last.then_inc(u.s_bef, 1)
                pe.wait_ge(u.s_rec, 1)
                if f:
                    pe.wait_ge(B[f - 1].s_R, 2)
                for t in range(ph.tiles):
                    pe.wait_ge(u.s_hot, t + 1)
                    for k in range(BLOCKS):
                        last = pe.matmul(recs[:, k, :], hot[:, t, k * P:(k + 1) * P],
                                         rec[:, ph.lo + t, :], start=(t == 0 and k == 0),
                                         stop=(t == ph.tiles - 1), skip_group_check=True)
                    last.then_inc(u.s_put, 1)

            def base_rows(g):
                if g == 0:
                    pe.wait_ge(s_x, 16)
                    pe.wait_ge(s_wti, 1)
                    pe.wait_ge(s_bp, 1)
                for k in range(4):
                    last = pe.transpose(ps_o[:, 1, k * P:(k + 1) * P], xs[:, 4 * g + k, :], ident)
                last.then_inc(s_bt, 1)
                if g:
                    pe.wait_ge(s_bc, g)
                for i in range(3):
                    pe.matmul(ps_o[:, 0, :], oneb[:], bparts[:, i].rearrange("p k d -> p (k d)"),
                              start=(i == 0), stop=False, skip_group_check=True)
                pe.wait_ge(s_btc, g + 1)
                for k in range(4):
                    last = pe.matmul(ps_o[:, 0, k * D:(k + 1) * D], xT[:, (4 * g + k) * P:(4 * g + k + 1) * P],
                                     wTi[:], start=False, stop=True, skip_group_check=True)
                last.then_inc(s_bo, 1)

            def block0(f):
                u = B[f]
                if f:
                    pe.wait_ge(B[0].s_lraw, 2)
                for j in range(SIDE):
                    pe.wait_ge(u.s_g[j], 16)
                    last = pe.transpose(ps_t[:, j // 4, (j % 4) * P:(j % 4 + 1) * P], u.G[:, j, :], ident)
                    if j in (3, SIDE - 1):
                        last.then_inc(u.s_lt, 1)
                pe.wait_ge(u.s_dw, 1)
                if f:
                    pe.wait_ge(B[0].s_aggL, 1)
                pe.matmul(lweight(), hc[0:LSLOTS, H_ONES:H_ONES + P], u.diagw[:],
                          start=True, stop=True).then_inc(u.s_lw, 1)

            def turn(e):
                f, k = ENDS[e]
                pe.wait_ge(B[f].s_agg[k - 1], 1)
                if e:
                    pe.wait_ge(s_ac, turn_of(e) - 1)
                pe.transpose(turned, B[f].agg[:, k - 1, :], ident).then_inc(s_at, 1)

            for t in range(NT):
                mask_made(pe, t)
                if t >= 2:
                    pe.wait_ge(s_word, t - 1)
                for q in range(BITS):
                    pe.matmul(ps_code[:, t % 2, :], hc[:, H_DIAG + q * P:H_DIAG + (q + 1) * P],
                              mask[:, t % MASKS, q * GROUPS:(q + 1) * GROUPS], start=(q == 0), stop=False)
                pe.matmul(ps_code[:, t % 2, :], hc[:, H_ID:H_ID + P], hc[:, H_GRP:H_GRP + GROUPS],
                          start=False, stop=True).then_inc(s_code, 1)
                if t == 1:
                    pe.wait_ge(s_c, 16)
                    pe.wait_ge(s_w, 16)
                    pe.transpose(ps_t[:, 0, 0:D], wsb[:], ident).then_inc(s_wt, 1)
                if t == PHASES[0].hi:
                    compact(0)
            compact(1)
            base_rows(0)
            block0(0)
            base_rows(1)
            pe.wait_ge(s_fb, 2)
            pe.wait_ge(B[1].s_R, 2)
            pe.matmul(fbcount, hc[:, H_ONES:H_ONES + P], fb[:], start=True, stop=True).then_inc(s_fbc, 1)
            base_rows(2)
            pe.wait_ge(s_word, NT)
            turn(0)
            turn(1)
            base_rows(3)
            block0(1)
            pe.wait_ge(s_bc, 4)
            pe.wait_ge(s_fbn, 1)
            def turn_own(e):
                pe.wait_ge(s_own[e], 16)
                if e:
                    pe.wait_ge(s_oc, e)
                pe.transpose(ps_o[:, 0, 0:P], own[:, e, :], ident).then_inc(s_ot, 1)

            def own_part(e):
                if e >= len(finish):
                    pe.wait_ge(s_yc, e + 1 - len(finish))
                for i in range(3):
                    pe.matmul(finish[e % len(finish)], oneb[:], bparts[:, i, 0, :], start=(i == 0), stop=False)
                pe.wait_ge(s_oc, e + 1)
                pe.matmul(finish[e % len(finish)], ownT[:, e, :], wTi[:], start=False, stop=False)

            def agg_part(e):
                if e == LX:
                    pe.wait_ge(B[1].s_aggL, 1)
                else:
                    pe.wait_ge(s_ac, turn_of(e))
                pe.matmul(finish[e % len(finish)], aggT[:, e, :], wT[:], start=False, stop=True).then_inc(s_y, 1)

            for e in (0, 1):
                turn_own(e)
                own_part(e)
                agg_part(e)
            turn(2)
            turn_own(2)
            own_part(2)
            agg_part(2)
            for e in (3, 4):
                turn_own(e)
                own_part(e)
            agg_part(3)
            turn(4)
            agg_part(4)

            n = pe.value_load(fbn[0:1, 0:1], min_val=0, max_val=N)
            with pe.If(n > 0):
                pe.matmul(fbfront, hc[:, H_TRI:H_TRI + P], fb[:], start=True, stop=False)
                for t in range(NT - 1):
                    last = pe.matmul(fbfront[:, t + 1:NT], hc[:, H_ONES:H_ONES + P],
                                     fb[:, t:t + 1].to_broadcast([P, NT - 1 - t]), start=False, stop=(t == NT - 2))
                last.then_inc(s_fpre, 1)
                with pe.Fori(0, n) as i:
                    pe.wait_ge(s_fc, i + 1)
                    pe.matmul(fout, fcol[:], wT[:], start=True, stop=False)
                    pe.matmul(fout, fxcol[:], wTi[:], start=False, stop=False)
                    pe.matmul(fout, onerow[:, 0:1], brow[:], start=False, stop=True).then_inc(s_fp, 1)

        @block.vector
        def _(dve):
            V = nc.vector
            steps = [0]

            def step(instruction):
                steps[0] += 1
                return instruction.then_inc(s_v, 1)

            def settle():
                dve.wait_ge(s_v, steps[0])

            V.memset(onerow[:], 1.0).then_inc(s_one, 1)
            V.memset(oneb[:], 1.0)

            def make_mask(t):
                dve.wait_ge(s_adj[t], 16)
                if t >= MASKS:
                    dve.wait_ge(s_code, t - MASKS + 1)
                    dve.wait_ge(s_cnt[(t - MASKS) in ACT_TILES], made(t - MASKS))
                V.tensor_scalar(mask[:, t % MASKS, :], A[:, t % RING, :], 0.0, None, ALU.not_equal).then_inc(s_mask, 1)

            def search(t):
                dve.wait_ge(s_code, t + 1)
                for q in range(QUARTERS):
                    last = V.max(codes[:, t, 8 * q:8 * q + 8], ps_code[:, t % 2, q * GQ:(q + 1) * GQ])
                last.then_inc(s_word, 1)

            def const(ph, at):
                return cc[:, at:at + 4].unsqueeze(2).to_broadcast([P, 4, ph.tiles])

            def classify(f):
                ph, u = PHASES[f], B[f]
                r = slice(ph.lo, ph.hi)
                wide = [P, 4, ph.tiles]
                dve.wait_ge(s_word, ph.hi)
                dve.wait_ge(s_cnt[0], made(ph.hi - 1) if ph.hi - 1 not in ACT_TILES else ph.hi - made(ph.hi - 1))
                if any(t in ACT_TILES for t in range(ph.hi)):
                    dve.wait_ge(s_cnt[1], sum(t in ACT_TILES for t in range(ph.hi)))
                n_row = cnt[:, r].unsqueeze(1).to_broadcast(wide)
                step(V.tensor_tensor(u.ge[:], n_row, const(ph, C_LEAST), ALU.is_ge))
                step(V.tensor_tensor(u.le[:], n_row, const(ph, C_MOST), ALU.is_le))
                eighth = codes[:, r].rearrange("p t (q e) -> p t q e", e=8)[:, :, :, 7]
                step(V.tensor_reduce(full[:, r], eighth, AX.X, ALU.max))
                settle()
                step(V.tensor_tensor(u.ge[:], u.ge[:], u.le[:], ALU.mult))
                step(V.tensor_scalar(ok[:, r], full[:, r], float(GROUPS), None, ALU.is_lt))
                settle()
                V.tensor_tensor(u.cls[:], u.ge[:], ok[:, r].unsqueeze(1).to_broadcast(wide), ALU.mult).then_inc(u.s_cls, 1)
                V.tensor_single_scalar(part[:, r, 0, :], codes[:, r], GROUPS - 1, ALU.bitwise_and)
                V.tensor_single_scalar(part[:, r, 1, :], codes[:, r], 9, ALU.logical_shift_right).then_inc(u.s_part, 1)

            def place(f):
                ph, u = PHASES[f], B[f]
                r = slice(ph.lo, ph.hi)
                dve.wait_ge(u.s_cls, 1)
                dve.wait_ge(u.s_bef, 1)
                step(V.tensor_tensor(u.le[:], before(ph), const(ph, C_CAP + 8 * f), ALU.is_lt))
                step(V.tensor_tensor(u.at[:], before(ph), const(ph, C_CAP + 8 * f + 4), ALU.add))
                settle()
                step(V.tensor_tensor(u.fits[:], u.le[:], u.cls[:], ALU.mult))
                settle()
                step(V.tensor_tensor(u.at[:], u.at[:], u.fits[:], ALU.mult))
                settle()
                step(V.tensor_reduce(slot[:, r], u.at[:].rearrange("p c t -> p t c"), AX.X, ALU.add))
                settle()
                if f:
                    dve.wait_ge(B[f - 1].s_put, PHASES[f - 1].tiles)
                for t in range(ph.tiles):
                    V.tensor_scalar(hot[:, t, :], hc[:, H_SLOT:H_END],
                                    slot[:, ph.lo + t:ph.lo + t + 1], None, ALU.is_equal).then_inc(u.s_hot, 1)

            def left_over(f):
                ph, u = PHASES[f], B[f]
                r = slice(ph.lo, ph.hi)
                step(V.tensor_reduce(placed[:, r], u.fits[:].rearrange("p c t -> p t c"), AX.X, ALU.add))
                settle()
                V.scalar_tensor_tensor(fb[:, r], cnt[:, r], float(LEAST[0]), placed[:, r], ALU.is_ge,
                                       ALU.subtract).then_inc(s_fb, 1)

            def decode(u, blocks):
                dve.wait_ge(u.s_R, 1)
                for q in range(BITS):
                    step(V.tensor_scalar(u.bit[:, q, blocks], u.bits[:, blocks], q, 1,
                                         ALU.logical_shift_right, ALU.bitwise_and))
                settle()
                dve.wait_ge(u.s_R, 2)
                for q in range(BITS):
                    step(V.scalar_tensor_tensor(u.keys[:, blocks, q, :], u.R[:, blocks, 0:WORDS],
                                                float(1 + GROUPS * (BITS - 1 - q)), u.bit[:, q, blocks],
                                                ALU.add, ALU.mult))

            def neighbours_lx(f):
                u = B[f]
                decode(u, slice(0, 1))
                n_slot = u.R[:, 0, 2 * WORDS + 2:2 * WORDS + 3]
                step(V.tensor_scalar(u.eq[:], cc[:, C_LO:C_LO + 4], n_slot, None, ALU.is_equal))
                step(V.tensor_scalar(u.lv[:], cc[:, C_V:C_V + 8], n_slot, None, ALU.is_le))
                settle()
                V.scalar_tensor_tensor(u.em[:], cc[:, C_HI:C_HI + 4], n_slot, u.eq[:], ALU.is_equal,
                                       ALU.add).then_inc(u.s_em, 1)
                keys = u.keys[:, 0].rearrange("p b w -> p (b w)")
                step(V.max(u.top[:, 0, :], keys))
                settle()
                dve.wait_ge(u.s_em, 1)
                step(V.match_replace(u.keyr[:], u.top[:, 0, :], keys, 0.0))
                settle()
                step(V.max(u.top[:, 1, :], u.keyr[:]))
                settle()
                tl = u.top[:, 0:2, :].rearrange("p a b -> p (a b)")
                h = LSLOTS
                step(V.tensor_scalar(u.lk[h:P, 0, :], tl[h:P, 5:13], u.em[h:P, 0:1], None, ALU.mult))
                step(V.tensor_tensor(u.lkv[0:h, :], tl[0:h, 0:8], u.lv[0:h, :], ALU.mult))
                for i in range(1, 4):
                    settle()
                    step(V.scalar_tensor_tensor(u.lk[h:P, i, :], tl[h:P, 5 + i:13 + i], u.em[h:P, i:i + 1],
                                                u.lk[h:P, i - 1, :], ALU.mult, ALU.add))
                settle()
                step(V.tensor_tensor(u.lkv[h:P, :], u.lk[h:P, 3, :], u.lv[h:P, :], ALU.mult))
                settle()
                V.tensor_scalar(u.nbL[:], u.lkv[:], -1.0, float(N), ALU.mult, ALU.add).then_inc(u.s_nbL, 1)

            def neighbours_ms(f):
                u = B[f]
                decode(u, slice(1, BLOCKS))
                settle()
                for k in range(1, BLOCKS):
                    step(V.max(u.top[:, 1 + k, :], u.keys[:, k].rearrange("p b w -> p (b w)")))
                settle()
                V.tensor_scalar(u.nb[:], u.top[:, 2:, :], -1.0, float(N), ALU.mult, ALU.add).then_inc(u.s_nb, 1)

            def rows(f):
                u = B[f]
                step(V.scalar_tensor_tensor(u.rid[:], u.R[:, :, 2 * WORDS], float(P), u.R[:, :, 2 * WORDS + 1],
                                            ALU.mult, ALU.add))
                step(V.tensor_scalar(u.none[:], u.R[:, :, 2 * WORDS + 2], 0.0, float(2 * N), ALU.is_equal, ALU.mult))
                settle()
                side = slice(f * LSLOTS, (f + 1) * LSLOTS)
                V.tensor_tensor(endrow[side, LX:LX + 1], u.rid[side, 0:1], u.none[side, 0:1], ALU.add)
                ms = slice(2, 5, 2) if f else slice(0, 2)
                V.tensor_tensor(endrow[:, ms], u.rid[:, 1:], u.none[:, 1:],
                                ALU.add).then_inc(s_endrow, 1)

            def classes_lx(f):
                ph, u = PHASES[f], B[f]
                n, lc = LUSED, ph.lcap
                dve.wait_ge(u.s_lraw, 2)
                raw = u.Lraw[:].rearrange("p j c r -> p r j c")
                for i in range(n):
                    step(V.max(u.small[:, i, :], raw[:, i]))
                for i in range(n - lc):
                    step(V.max(u.large[:, i, :], u.xpos[:, :, i]))
                settle()

                def rank(k, xs):
                    return u.small[:, lc:n, k] if xs else u.small[:, 0:lc, k]

                def rank_from_top(k):
                    return u.large[:, :, 2 * SIDE - 1 - k]

                for i, (a, b, xs) in enumerate(((1, 3, 0), (2, 4, 0), (2, 5, 1), (3, 6, 1))):
                    o = u.sumt[:, i % 2, lc:n] if xs else u.sumt[:, i % 2, 0:lc]
                    step(V.tensor_tensor(o, rank(a, xs), rank(b, xs), ALU.add))
                settle()
                step(V.tensor_tensor(u.sums[:, 0, 0:lc], u.sumt[:, 0, 0:lc], rank(5, 0), ALU.add))
                step(V.tensor_tensor(u.sums[:, 1, 0:lc], u.sumt[:, 1, 0:lc], rank(7, 0), ALU.add))
                step(V.tensor_tensor(u.sums[:, 0, lc:n], u.sumt[:, 0, lc:n], rank_from_top(8), ALU.subtract))
                step(V.tensor_tensor(u.sums[:, 1, lc:n], u.sumt[:, 1, lc:n], rank_from_top(10), ALU.subtract))
                settle()
                dve.wait_ge(u.s_lw, 1)
                lw = lweight()
                step(V.tensor_tensor(u.sumt[:, :, 0:lc], lw[:, 0:2, 0:lc], u.sums[:, :, 0:lc], ALU.mult))
                step(V.tensor_tensor(u.sumt[:, :, lc:n], lw[:, 2:4, lc:n], u.sums[:, :, lc:n], ALU.mult))
                settle()
                V.scalar_tensor_tensor(aggT[:, LX, f * LSLOTS:f * LSLOTS + n], u.sumt[:, 0, :], -1.0, u.sumt[:, 1, :], ALU.mult,
                                       ALU.subtract).then_inc(u.s_aggL, 1)

            def class_s(f):
                u = B[f]
                for g in range(G_S, NG):
                    dve.wait_ge(u.s_g[g], 16)
                a, b = u.G[:, G_S:NG:2, :], u.G[:, G_S + 1:NG:2, :]
                step(V.tensor_tensor(s4[:, 0:2], a, b, ALU.min))
                step(V.tensor_tensor(s4[:, 2:4], a, b, ALU.max))
                settle()
                step(V.tensor_tensor(s4[:, 4], s4[:, 2], s4[:, 3], ALU.min))
                step(V.tensor_tensor(s4[:, 5], s4[:, 0], s4[:, 1], ALU.add))
                settle()
                V.tensor_tensor(u.agg[:, 1], s4[:, 4], s4[:, 5], ALU.add).then_inc(u.s_agg[1], 1)
                dve.wait_ge(u.s_agg[1], 1)

            def class_m(f):
                u = B[f]
                for g in range(G_M, G_S):
                    dve.wait_ge(u.s_g[g], 16)

                def two(i, j):
                    return scr[:, i:j + 1:j - i, :]

                a, b = u.G[:, G_M:G_M + 3, :], u.G[:, G_M + 3:G_S, :]
                step(V.tensor_tensor(scr[:, 0:3, :], a, b, ALU.min))
                step(V.tensor_tensor(scr[:, 6:9, :], a, b, ALU.max))
                settle()
                step(V.tensor_tensor(two(3, 4), two(1, 7), two(2, 8), ALU.min))
                step(V.tensor_tensor(two(9, 10), two(1, 7), two(2, 8), ALU.max))
                settle()
                step(V.tensor_tensor(two(1, 2), two(0, 9), two(4, 6), ALU.min))
                step(V.tensor_tensor(two(5, 7), two(0, 9), two(4, 6), ALU.max))
                settle()
                step(V.tensor_tensor(two(0, 4), two(1, 2), two(3, 5), ALU.max))
                step(V.tensor_tensor(two(6, 8), two(2, 10), two(5, 7), ALU.min))
                settle()
                step(V.tensor_tensor(scr[:, 9], scr[:, 4], scr[:, 8], ALU.max))
                step(V.tensor_tensor(scr[:, 11], scr[:, 0], scr[:, 6], ALU.add))
                settle()
                V.tensor_tensor(u.agg[:, 0], scr[:, 9], scr[:, 11], ALU.add).then_inc(u.s_agg[0], 1)
                dve.wait_ge(u.s_agg[0], 1)

            def tile(t):
                if t + 2 < NT and t + 2 not in ACT_TILES:
                    make_mask(t + 2)
                search(t)

            make_mask(0)
            make_mask(1)
            for t in range(PHASES[0].hi):
                tile(t)
                if t != 2:
                    continue
                dve.wait_ge(s_wc, 1)
                V.scalar_tensor_tensor(wTi[:], wT[:], 0.5, cc[:, C_ID:C_ID + P], ALU.mult, ALU.add).then_inc(s_wti, 1)
                dve.wait_ge(s_b, 16)
                for k in range(4):
                    step(V.tensor_copy(b4[:, k, :], brow[:]))
                settle()
                left = b4[:]
                for i in range(2):
                    step(V.tensor_copy(bparts[:, i], left))
                    settle()
                    step(V.tensor_tensor(bleft[:, i], left, bparts[:, i], ALU.subtract))
                    settle()
                    left = bleft[:, i]
                V.tensor_copy(bparts[:, 2], left).then_inc(s_bp, 1)
            second = iter(range(PHASES[0].hi, NT))
            classify(0)
            tile(next(second))
            place(0)
            tile(next(second))
            neighbours_lx(0)
            tile(next(second))
            neighbours_ms(0)
            for t in second:
                tile(t)
            classify(1)
            place(1)
            left_over(0)
            left_over(1)
            neighbours_ms(1)
            neighbours_lx(1)
            rows(0)
            rows(1)
            class_m(0)
            class_s(0)
            dve.wait_ge(s_fill, 1)
            classes_lx(0)
            class_m(1)
            classes_lx(1)
            class_s(1)

            dve.wait_ge(s_fbn, 1)
            n = dve.value_load(fbn[0:1, 0:1], min_val=0, max_val=N)
            with dve.If(n > 0):
                is_nb, rnk = A[:, 1, :].bitcast(F32), A[:, 2, :].bitcast(F32)
                kept, vals, below = A[:, 3, :], A[:, 4, :].bitcast(F32), A[:, 5, :].bitcast(F32)
                ones = A[:, 6, :].bitcast(F32)
                V.memset(ones, 1.0)
                tp = hc[:, H_TP:H_SLOT].rearrange("p (t a) -> p t a", a=2)
                dve.wait_ge(s_fpre, 1)
                V.tensor_scalar(fbpos[:], fb[:], -2.0 * N, 2.0 * N, ALU.mult, ALU.add)
                dve.drain()
                V.tensor_tensor(fbat[:], fbpos[:], fbfront, ALU.add)
                V.scalar_tensor_tensor(fbrow[:], tp[:, :, 0], float(P), tp[:, :, 1], ALU.mult, ALU.add).then_inc(s_fat, 1)
                dve.wait_ge(s_list, 16 * NT)
                with dve.Fori(0, n) as i:
                    row = dve.value_load(rowlist[bass.ds(i, 1), :], min_val=0, max_val=N - 1)
                    V.tensor_copy(fxcol[:], xT[:, bass.ds(row, 1)])
                    V.memset(vals, BIG)
                    V.memset(fpre[:], 0)
                    V.memset(fbit[:], -2**31)
                    dve.wait_ge(s_fa, i * 16 + 16)
                    V.tensor_scalar(is_nb, A[:, 0, :], 0.0, None, ALU.not_equal)
                    dve.drain()
                    V.tensor_tensor_scan(rnk, ones, is_nb, 0.0, ALU.mult, ALU.add)
                    dve.drain()
                    V.tensor_scalar(fm[:, 1:2], rnk[:, N - 1:N], 0.5, 0.25, ALU.mult, ALU.add)
                    dve.drain()
                    V.tensor_scalar(fm[:, 0:1], fm[:, 1:2], MAGIC, -MAGIC, ALU.add, ALU.add)
                    dve.drain()
                    V.tensor_scalar(fm[:, 1:2], fm[:, 0:1], 2.0, None, ALU.mult)
                    V.scalar_tensor_tensor(is_nb, rnk, fm[:, 0:1], is_nb, ALU.not_equal, ALU.mult)
                    for j, q in enumerate((0.25, 0.5, 0.75)):
                        V.tensor_scalar(fk[:, j:j + 1], fm[:, 0:1], 2 * q, 0.375 - 2 * q, ALU.mult, ALU.add)
                    dve.drain()
                    V.scalar_tensor_tensor(kept, rnk, fm[:, 1:2], is_nb, ALU.not_equal, ALU.mult)
                    V.tensor_scalar(fcnt[:], fk[:], MAGIC, -MAGIC, ALU.add, ALU.add)
                    dve.drain()
                    V.copy_predicated(vals, kept, xT[:])
                    V.tensor_scalar(fk[:], fcnt[:], -1.0, None, ALU.add)
                    dve.drain()
                    with dve.Fori(0, 32):
                        V.tensor_tensor(fcand[:], fpre[:], fbit[:], ALU.bitwise_or)
                        dve.drain()
                        V.tensor_scalar(fsgn[:], fcand[:], 31, -1, ALU.arith_shift_right, ALU.bitwise_xor)
                        dve.drain()
                        V.scalar_tensor_tensor(fval[:], fsgn[:], -2**31, fcand[:], ALU.bitwise_or, ALU.bitwise_xor)
                        dve.drain()
                        for j in range(3):
                            V.tensor_scalar(below, vals, fval[:, j:j + 1].bitcast(F32), None, ALU.is_lt, ALU.add,
                                            accum_out=fcnt[:, j:j + 1])
                            dve.drain()
                        V.tensor_tensor(ftake[:], fcnt[:], fk[:], ALU.is_le)
                        dve.drain()
                        V.copy_predicated(fpre[:], ftake[:], fcand[:])
                        dve.drain()
                        V.tensor_single_scalar(fbit[:], fbit[:], 1, ALU.logical_shift_right)
                        dve.drain()
                    V.tensor_scalar(fsgn[:], fpre[:], 31, -1, ALU.arith_shift_right, ALU.bitwise_xor)
                    dve.drain()
                    V.scalar_tensor_tensor(fval[:], fsgn[:], -2**31, fpre[:], ALU.bitwise_or, ALU.bitwise_xor)
                    dve.drain()
                    V.tensor_scalar(fcnt[:], fval[:].bitcast(F32), THIRD / 2, None, ALU.mult)
                    dve.drain()
                    V.tensor_reduce(fcol[:], fcnt[:], AX.X, ALU.add).then_inc(s_fc, 1)
                    dve.wait_ge(s_fp, i + 1)
                    V.tensor_copy(frow[:], fout).then_inc(s_fy, 1)


def kernel(x, adj, L0_gnn_W, L0_gnn_b):
    import concourse.bacc as bacc
    from concourse.bass_utils import run_bass_kernel_spmd as run

    nc = bacc.Bacc("TRN2", target_bir_lowering=False, num_devices=1)
    hconst, cconst = constants()
    arrays = {
        "x_dram": np.ascontiguousarray(x),
        "adj_dram": np.ascontiguousarray(adj),
        "w_dram": np.ascontiguousarray(L0_gnn_W),
        "b_dram": np.ascontiguousarray(L0_gnn_b).reshape(1, D),
        "hconst_dram": hconst,
        "cconst_dram": cconst,
    }
    args = [nc.dram_tensor(k, a.shape, mybir.dt.from_np(a.dtype), kind="ExternalInput").ap()
            for k, a in arrays.items()]
    out = nc.dram_tensor("out_dram", (N, D), F32, kind="ExternalOutput").ap()
    build(nc, *args, out)
    return run(nc, [arrays], core_ids=[0]).results[0]["out_dram"]
```

```python
from contextlib import ExitStack

import numpy as np
import concourse.bass as bass
from concourse import mybir

F32 = mybir.dt.float32
F16 = mybir.dt.float16
BF16 = mybir.dt.bfloat16
I32 = mybir.dt.int32
U32 = mybir.dt.uint32
ALU = mybir.AluOpType
ACT = mybir.ActivationFunctionType
AX = mybir.AxisListType

P = 128
N = 2048
D = 128
NT = N // P
BITS = 4
GROUPS = N // BITS
QUARTERS = 4
GQ = GROUPS // QUARTERS
WORDS = 8 * QUARTERS
BIG = float(np.finfo(np.float32).max)
THIRD = float(np.float32(1.0 / 3.0))
MAGIC = float(3 << 22)

S, M, L, X = range(4)
LEAST, MOST = (6, 7, 9, 13), (6, 8, 12, 16)
M_RANKS = (0, 1, 2, 4, 5, 6)
S_RANKS = (0, 1, 3, 4)
MR, SR = len(M_RANKS), len(S_RANKS)
SIDE = 7


class Phase:

    def __init__(self, lo, hi, xcap):
        self.lo, self.hi, self.tiles = lo, hi, hi - lo
        self.caps = (P, P, LUSED - xcap, xcap)
        self.lcap = LUSED - xcap


LSLOTS = P // 2
LUSED = 38
BLOCKS = 3
G_M, G_S = SIDE, SIDE + MR
NG = SIDE + MR + SR
PHASES = (Phase(0, NT // 2, 3), Phase(NT // 2, NT, 3))
OFFS = lambda ph: (2 * P, P, 0, ph.lcap)
ACT_TILES = (9, 12)
FIELDS = 2 * WORDS + 3
MASKS = 4
RING = 8

H_ID, H_TRI, H_TP, H_END = np.cumsum([0, P, P, 2 * NT]).tolist()
C_LEAST, C_MOST, C_LO, C_HI, C_V, C_CAP = np.cumsum([0, 4, 4, 4, 4, SIDE + 1]).tolist()
C_END = C_CAP + 16


def constants():
    h = np.zeros((P, H_END), np.float16)
    eye = np.eye(P)
    h[:, H_ID:H_TRI] = eye
    h[:, H_TRI:H_TP] = np.triu(np.ones((P, P)), 1)
    tp = np.zeros((P, NT, 2))
    tp[:, :, 0] = np.arange(NT)
    tp[:, :, 1] = np.arange(P)[:, None]
    h[:, H_TP:] = tp.reshape(P, -1)
    c = np.zeros((P, C_END), np.float32)
    c[:, C_LEAST:C_MOST] = LEAST
    c[:, C_MOST:C_LO] = MOST
    c[:, C_LO:C_HI] = (9, 11, 13, 15)
    c[:, C_HI:C_V] = (10, 12, 14, 16)
    c[:, C_V:C_CAP] = 2 * np.arange(SIDE + 1) + 3
    for f, ph in enumerate(PHASES):
        c[:, C_CAP + 8 * f:C_CAP + 8 * f + 4] = ph.caps
        c[:, C_CAP + 8 * f + 4:C_CAP + 8 * f + 8] = np.array(OFFS(ph)) + 1
    return h, c


def build(nc, x, adj, w, b, hconst, cconst, out):
    ctx = ExitStack()
    with ctx:
        def sb(name, shape, dt):
            return ctx.enter_context(nc.sbuf_tensor(name, shape, dt))

        def pb(name, shape, dt):
            return ctx.enter_context(nc.psum_tensor(name, shape, dt))

        def sem(name):
            return ctx.enter_context(nc.semaphore(name))

        A = sb("A", [P, RING, N], I32)
        mask = sb("mask", [P, MASKS, N], F16)
        junk = sb("junk", [P, 2, N], F16)
        hc = sb("hc", [P, H_END], F16)
        cc = sb("cc", [P, C_END], F32)
        diags = sb("diags", [P, BITS, P], F16)
        ones = sb("ones", [P, P], F16)
        groups = sb("groups", [P, GROUPS], F16)
        slots = sb("slots", [P, BLOCKS * P], F16)
        ident = sb("ident", [P, P], F32)
        xs = sb("xs", [P, NT, D], F32)
        xT = sb("xT", [P, N], F32)
        base = sb("base", [P, NT, D], F32)
        wsb = sb("wsb", [P, D], F32)
        wT = sb("wT", [P, D], F32)
        wTi = sb("wTi", [P, D], F32)
        brow = sb("brow", [1, D], F32)
        b4 = sb("b4", [1, 4, D], F32)
        bleft = sb("bleft", [1, 2, 4, D], F32)
        bparts = sb("bparts", [1, 3, 4, D], BF16)
        oneb = sb("oneb", [1, P], BF16)
        onerow = sb("onerow", [1, P], F32)
        codes = sb("codes", [P, NT, WORDS], I32)
        part = sb("part", [P, NT, 2, WORDS], I32)
        rec = sb("rec", [P, NT, FIELDS], F16)
        cnt = sb("cnt", [P, NT], F32)
        full = sb("full", [P, NT], F32)
        ok = sb("ok", [P, NT], F32)
        placed = sb("placed", [P, NT], F32)
        slot = sb("slot", [P, NT], F32)
        fb = sb("fb", [P, NT], F16)

        hot = sb("hot", [P, max(ph.tiles for ph in PHASES), BLOCKS * P], F16)

        class Bufs:

            def __init__(self, f, ph):
                def own(name, shape, dt):
                    return sb(f"{name}{f}", shape, dt)

                nb = BLOCKS
                self.ge = own("ge", [P, 4, ph.tiles], F32)
                self.le = own("le", [P, 4, ph.tiles], F32)
                self.cls = own("cls", [P, 4, ph.tiles], F16)
                self.fits = own("fits", [P, 4, ph.tiles], F32)
                self.at = own("at", [P, 4, ph.tiles], F32)
                self.R = own("R", [P, nb, FIELDS], F32)
                self.rid = own("rid", [P, nb], F32)
                self.none = own("none", [P, nb], F32)
                self.bits = own("bits", [P, nb, WORDS], I32)
                self.bit = own("bit", [P, BITS, nb, WORDS], I32)
                self.keys = own("keys", [P, nb, BITS, WORDS], F32)
                self.keyr = own("keyr", [P, BITS * WORDS], F32)
                self.top = own("top", [P, nb + 1, 8], F32)
                self.eq = own("eq", [P, 4], F32)
                self.em = own("em", [P, 4], F32)
                self.lv = own("lv", [P, 8], F32)
                self.lk = own("lk", [P, 4, 8], F32)
                self.lkv = own("lkv", [P, 8], F32)
                self.nbL = own("nbL", [P, 8], I32)
                self.nb = own("nb", [P, nb - 1, 8], I32)
                self.G = own("G", [P, NG, D], F32)
                self.diagw = own("diagw", [LSLOTS, 4, LUSED], F16)
                self.Lraw = own("Lraw", [P, SIDE, 2, LUSED], F32)
                self.small = own("small", [P, LUSED, 8], F32)
                xcap = LUSED - ph.lcap
                self.xpos = own("xpos", [P, 2 * SIDE, xcap], F32)
                self.large = own("large", [P, xcap, 8], F32)
                self.sums = own("sums", [P, 2, LUSED], F32)
                self.sumt = own("sumt", [P, 2, LUSED], F32)
                self.agg = own("agg", [P, 2, D], F32)
                self.s_part = sem(f"s_part{f}")
                self.s_rec = sem(f"s_rec{f}")
                self.s_cls = sem(f"s_cls{f}")
                self.s_bef = sem(f"s_bef{f}")
                self.s_hot = sem(f"s_hot{f}")
                self.s_put = sem(f"s_put{f}")
                self.s_R = sem(f"s_R{f}")
                self.s_nbL = sem(f"s_nbL{f}")
                self.s_nb = sem(f"s_nb{f}")
                self.s_fill = sem(f"s_fill{f}")
                self.s_g = [sem(f"s_g{f}_{g}") for g in range(NG)]
                self.s_em = sem(f"s_em{f}")
                self.s_dw = sem(f"s_dw{f}")
                self.s_lw = sem(f"s_lw{f}")
                self.s_lt = sem(f"s_lt{f}")
                self.s_lraw = sem(f"s_lraw{f}")
                self.s_agg = [sem(f"s_agg{f}_{k}") for k in range(2)]
                self.s_aggL = sem(f"s_aggL{f}")

        B = [Bufs(f, ph) for f, ph in enumerate(PHASES)]
        scr = sb("scr", [P, 12, D], F32)
        s4 = sb("s4", [P, 6, D], F32)
        ENDS = ((0, 1), (0, 2), (1, 1), (None, 0), (1, 2))
        ends = range(len(ENDS))
        LX = ENDS.index((None, 0))
        aggT = sb("aggT", [P, len(ENDS), P], F32)
        endrow = sb("endrow", [P, len(ENDS)], I32)
        own = sb("own", [P, len(ENDS), D], F32)
        ownT = sb("ownT", [P, len(ENDS), P], F32)
        y = sb("y", [P, len(ENDS), D], F32)
        fbn = sb("fbn", [P, 1], I32)
        fbnf = sb("fbnf", [P, 1], F32)
        fbj = sb("fbj", [P, NT], F32)
        fbpos = sb("fbpos", [P, NT], F32)
        fbat = sb("fbat", [P, NT], I32)
        fbrow = sb("fbrow", [P, NT], I32)
        fm = sb("fm", [P, 2], F32)
        fk = sb("fk", [P, 3], F32)
        fcnt = sb("fcnt", [P, 3], F32)
        fpre = sb("fpre", [P, 3], I32)
        fbit = sb("fbit", [P, 3], I32)
        fcand = sb("fcand", [P, 3], I32)
        fsgn = sb("fsgn", [P, 3], I32)
        fval = sb("fval", [P, 3], I32)
        ftake = sb("ftake", [P, 3], I32)
        fcol = sb("fcol", [P, 1], F32)
        fxcol = sb("fxcol", [P, 1], F32)
        frow = sb("frow", [1, D], F32)
        rowlist = nc.dram_tensor("rowlist", (N, 1), I32, kind="Internal").ap()
        ps_code = pb("ps_code", [P, 2, GROUPS], F32)
        ps_misc = pb("ps_misc", [P, 512], F32)
        ps_rec = pb("ps_rec", [P, 512], F32)
        ps_t = pb("ps_t", [P, 2, 512], F32)
        ps_o = pb("ps_o", [P, 2, 512], F32)
        fbcount = ps_rec[:, 512 - NT:]
        fbfront = ps_misc[:, 96:96 + NT]
        fout = ps_misc[0:1, 128:128 + D]
        turned = ps_code[:, 1, 0:P]
        finish = [ps_code[:, 0, 0:D], ps_rec[:, 0:D], ps_o[:, 1, 0:D]]

        def before(ph):
            return ps_misc[:, 0:4 * ph.tiles].rearrange("p (c t) -> p c t", c=4)

        def lweight():
            return ps_misc[:, 256:256 + 4 * LUSED].rearrange("p (h r) -> p h r", h=4)

        recs = ps_rec[:, 0:BLOCKS * FIELDS].rearrange("p (k f) -> p k f", k=BLOCKS)

        s_adj = [sem(f"s_adj{t}") for t in range(NT)]
        s_h = sem("s_h")
        s_c = sem("s_c")
        s_w = sem("s_w")
        s_b = sem("s_b")
        s_x = sem("s_x")
        s_mask = sem("s_mask")
        s_amask = sem("s_amask")
        s_sign = sem("s_sign")
        s_bp = sem("s_bp")
        s_endrow = sem("s_endrow")
        s_own = [sem(f"s_own{e}") for e in ends]
        s_at = sem("s_at")
        s_ac = sem("s_ac")
        s_ot = sem("s_ot")
        s_oc = sem("s_oc")
        s_sc = sem("s_sc")
        s_code = sem("s_code")
        s_word = sem("s_word")
        s_cnt = [sem("s_cnt"), sem("s_acnt")]
        s_v = sem("s_v")
        s_wt = sem("s_wt")
        s_wc = sem("s_wc")
        s_wti = sem("s_wti")
        s_bt = sem("s_bt")
        s_btc = sem("s_btc")
        s_bo = sem("s_bo")
        s_bc = sem("s_bc")
        s_bst = sem("s_bst")
        s_y = sem("s_y")
        s_yc = sem("s_yc")
        s_one = sem("s_one")
        s_table = sem("s_table")
        s_diag = sem("s_diag")
        s_fill = sem("s_fill")
        s_fb = sem("s_fb")
        s_fbc = sem("s_fbc")
        s_fbf = sem("s_fbf")
        s_fbn = sem("s_fbn")
        s_fpre = sem("s_fpre")
        s_fat = sem("s_fat")
        s_list = sem("s_list")
        s_fa = sem("s_fa")
        s_fc = sem("s_fc")
        s_fp = sem("s_fp")
        s_fy = sem("s_fy")
        s_fo = sem("s_fo")
        s_fs = sem("s_fs")

        def turn_of(e):
            return e + 1 - (e > LX)

        def made(t):
            return sum((i in ACT_TILES) == (t in ACT_TILES) for i in range(t + 1))

        def mask_made(engine, t):
            engine.wait_ge(s_amask if t in ACT_TILES else s_mask, made(t))

        def counted(engine, tiles):
            theirs = sum(t in ACT_TILES for t in range(tiles))
            engine.wait_ge(s_cnt[0], tiles - theirs)
            if theirs:
                engine.wait_ge(s_cnt[1], theirs)

        block = ctx.enter_context(nc.Block())

        @block.sync
        def _(sp):
            for t in range(NT):
                if t >= RING:
                    mask_made(sp, t - RING)
                if t == 0:
                    sp.dma_start(hc[:], hconst).then_inc(s_h, 16)
                sp.dma_start(A[:, t % RING, :], adj[t * P:(t + 1) * P, :]).then_inc(s_adj[t], 16)
                if t == 1:
                    sp.dma_start(cc[:], cconst).then_inc(s_c, 16)
                    sp.dma_start(wsb[:], w).then_inc(s_w, 16)
                    sp.dma_start(brow[:], b).then_inc(s_b, 16)
            sp.dma_start(xs[:], x.rearrange("(k p) d -> p k d", p=P)).then_inc(s_x, 16)
            out_t = out.rearrange("(g k p) d -> g p k d", k=4, p=P)
            for g in range(4):
                sp.wait_ge(s_bc, g + 1)
                sp.dma_start(out_t[g], base[:, 4 * g:4 * g + 4, :]).then_inc(s_bst, 16)
            sp.wait_ge(s_bst, 64)

            sp.wait_ge(s_fbn, 1)
            sp.wait_ge(s_sc, 16 * len(ENDS))
            n = sp.value_load(fbn[0:1, 0:1], min_val=0, max_val=N)
            with sp.If(n > 0):
                mask_made(sp, NT - 1)
                mask_made(sp, ACT_TILES[-1])
                sp.wait_ge(s_list, 16 * NT)
                with sp.Fori(0, n) as i:
                    row = sp.value_load(rowlist[bass.ds(i, 1), :], min_val=0, max_val=N - 1)
                    sp.dma_start(A[:, 0, :], adj[bass.ds(row, 1), :].to_broadcast([P, N])).then_inc(s_fa, 16)
                    sp.wait_ge(s_fy, i + 1)
                    sp.dma_start(out[bass.ds(row, 1), :], frow[:]).then_inc(s_fo, 16)
                    sp.wait_ge(s_fo, i * 16 + 16)
                    sp.sem_inc(s_fs, 1)

        @block.gpsimd
        def _(pool):
            iota = nc.gpsimd.iota
            iota(groups[:], [[-1, GROUPS]], base=GROUPS - 1, channel_multiplier=0,
                 allow_small_or_imprecise_dtypes=True).then_inc(s_table, 1)
            iota(slots[:, 0:P], [[0, 2], [1, LSLOTS]], base=1, channel_multiplier=0,
                 allow_small_or_imprecise_dtypes=True).then_inc(s_table, 1)
            iota(slots[:, P:], [[1, (BLOCKS - 1) * P]], base=P + 1, channel_multiplier=0,
                 allow_small_or_imprecise_dtypes=True).then_inc(s_table, 1)
            for u in B:
                nc.gpsimd.memset(u.G[:, 0:SIDE, :], BIG).then_inc(u.s_fill, 1)
                nc.gpsimd.memset(u.G[:, SIDE:, :], 0.0).then_inc(u.s_fill, 1)
            nc.gpsimd.memset(own[:], 0.0).then_inc(B[1].s_fill, 1)
            nc.gpsimd.memset(aggT[:, LX, :], 0.0).then_inc(s_fill, 1)

            def gather(to, source, index, done):
                nc.gpsimd.indirect_dma_start(
                    to, None, source[:, :], bass.IndirectOffsetOnAxis(ap=index.bitcast(U32), axis=0),
                    bounds_check=N - 1, oob_is_err=False).then_inc(done, 16)

            def gather_own(e):
                gather(own[:, e, :], x, endrow[:, e:e + 1], s_own[e])

            def gather_lx(u):
                pool.wait_ge(u.s_nbL, 1)
                for j in range(SIDE):
                    gather(u.G[:, j, :], x, u.nbL[:, j:j + 1], u.s_g[j])

            def gather_k(u, k, at, ranks):
                pool.wait_ge(u.s_nb, 1)
                for j, r in enumerate(ranks):
                    gather(u.G[:, at + j, :], x, u.nb[:, k, r:r + 1], u.s_g[at + j])

            pool.wait_ge(B[0].s_fill, 2)
            gather_k(B[0], 0, G_M, M_RANKS)
            gather_k(B[0], 1, G_S, S_RANKS)
            gather_lx(B[0])
            pool.wait_ge(B[1].s_fill, 3)
            pool.wait_ge(s_endrow, 1)
            gather_own(0)
            gather_own(1)
            gather_k(B[1], 0, G_M, M_RANKS)
            gather_lx(B[1])
            pool.wait_ge(s_endrow, 2)
            gather_own(2)
            gather_own(3)
            gather_k(B[1], 1, G_S, S_RANKS)
            gather_own(4)
            pool.wait_ge(s_bst, 64)
            for e in ends:
                pool.wait_ge(s_yc, e + 1)
                nc.gpsimd.indirect_dma_start(
                    out[:, :], bass.IndirectOffsetOnAxis(ap=endrow[:, e:e + 1].bitcast(U32), axis=0),
                    y[:, e, :], None, bounds_check=N - 1, oob_is_err=False).then_inc(s_sc, 16)
            pool.wait_ge(s_sc, 16 * len(ENDS))

            pool.wait_ge(s_fbn, 1)
            n = pool.value_load(fbn[0:1, 0:1], min_val=0, max_val=N)
            with pool.If(n > 0):
                pool.wait_ge(s_fat, 1)
                for t in range(NT):
                    nc.gpsimd.indirect_dma_start(
                        rowlist[:, :], bass.IndirectOffsetOnAxis(ap=fbat[:, t:t + 1].bitcast(U32), axis=0),
                        fbrow[:, t:t + 1], None, bounds_check=N - 1, oob_is_err=False).then_inc(s_list, 16)

        @block.scalar
        def _(act):
            copy = nc.scalar.copy
            act.wait_ge(s_h, 16)
            for q in range(BITS):
                nc.scalar.mul(diags[:, q, :], hc[:, H_ID:H_ID + P], float(GROUPS << q)).then_inc(s_diag, 1)
            copy(ident[:], hc[:, H_ID:H_ID + P]).then_inc(s_diag, 1)

            def record(f):
                ph, u = PHASES[f], B[f]
                r = slice(ph.lo, ph.hi)
                tp = hc[:, H_TP:].rearrange("p (t a) -> p t a", a=2)
                copy(rec[:, r, 2 * WORDS:2 * WORDS + 2], tp[:, r, :])
                counted(act, ph.hi)
                copy(rec[:, r, 2 * WORDS + 2], cnt[:, r])
                act.wait_ge(u.s_part, 1)
                copy(rec[:, r, 0:2 * WORDS], part[:, r].rearrange("p t a w -> p t (a w)")).then_inc(u.s_rec, 1)

            def compacted(f):
                ph, u = PHASES[f], B[f]
                act.wait_ge(u.s_put, ph.tiles)
                copy(u.bits[:], recs[:, :, WORDS:2 * WORDS]).then_inc(u.s_R, 1)
                copy(u.R[:], recs).then_inc(u.s_R, 1)

            def base_rows(g):
                act.wait_ge(s_bt, g + 1)
                copy(xT[:, g * 512:(g + 1) * 512], ps_o[:, 1, :]).then_inc(s_btc, 1)
                act.wait_ge(s_bo, g + 1)
                copy(base[:, 4 * g:4 * g + 4, :].rearrange("p k d -> p (k d)"), ps_o[:, 0, :]).then_inc(s_bc, 1)

            def weights(f):
                u = B[f]
                act.wait_ge(u.s_em, 1)
                for i in range(4):
                    last = nc.scalar.activation(u.diagw[:, i, :], hc[0:LSLOTS, H_ID:H_ID + LUSED], ACT.Copy,
                                                scale=u.em[0:LSLOTS, i:i + 1])
                last.then_inc(u.s_dw, 1)

            def block0(f):
                u = B[f]
                for c, k in enumerate((4, SIDE - 4)):
                    act.wait_ge(u.s_lt, c + 1)
                    sides = ps_t[:, c, 0:k * P].rearrange("p (j c r) -> p (j c) r", c=2, r=LSLOTS)
                    nc.scalar.activation(u.Lraw[:, 4 * c:4 * c + k].rearrange("p j c r -> p (j c) r"),
                                         sides[:, :, 0:LUSED], ACT.Copy, scale=-THIRD / 2)
                    nc.scalar.activation(u.xpos[:, 8 * c:8 * c + 2 * k, :], sides[:, :, PHASES[f].lcap:LUSED],
                                         ACT.Copy, scale=THIRD / 2).then_inc(u.s_lraw, 1)

            def turned_agg(e):
                act.wait_ge(s_at, turn_of(e))
                nc.scalar.activation(aggT[:, e, :], turned, ACT.Copy, scale=THIRD / 2).then_inc(s_ac, 1)

            def turned_own(e):
                act.wait_ge(s_ot, e + 1)
                copy(ownT[:, e, :], ps_o[:, 0, 0:P]).then_inc(s_oc, 1)

            def finished(e):
                act.wait_ge(s_y, e + 1)
                copy(y[:, e, :], finish[e % len(finish)]).then_inc(s_yc, 1)

            def make_mask(t):
                act.wait_ge(s_adj[t], 16)
                if t >= MASKS:
                    act.wait_ge(s_code, t - MASKS + 1)
                    act.wait_ge(s_cnt[(t - MASKS) in ACT_TILES], made(t - MASKS))
                m = mask[:, t % MASKS, :]
                n = made(t)
                nc.scalar.activation(m, A[:, t % RING, :], ACT.Sign).then_inc(s_sign, 1)
                act.wait_ge(s_sign, n)
                nc.scalar.activation(m, m, ACT.Square, accum_out=cnt[:, t:t + 1]).then_inc(s_cnt[1], 1)
                act.wait_ge(s_cnt[1], n)
                act.sem_inc(s_amask, 1)

            for t in range(NT):
                if t + 1 in ACT_TILES:
                    make_mask(t + 1)
                if t == PHASES[0].hi:
                    compacted(0)
                if t not in ACT_TILES:
                    mask_made(act, t)
                    n = made(t)
                    if n > 2:
                        act.wait_ge(s_cnt[0], n - 2)
                    nc.scalar.activation(junk[:, n % 2, :], mask[:, t % MASKS, :], ACT.Copy,
                                         accum_out=cnt[:, t:t + 1]).then_inc(s_cnt[0], 1)
                if t == 2:
                    act.wait_ge(s_wt, 1)
                    copy(wT[:], ps_t[:, 0, 0:D]).then_inc(s_wc, 1)
                if t == PHASES[0].hi - 1:
                    record(0)
            record(1)
            compacted(1)
            base_rows(0)
            weights(0)
            block0(0)
            weights(1)
            base_rows(1)
            act.wait_ge(s_fbc, 1)
            nc.scalar.activation(fbj[:], fbcount, ACT.Copy, accum_out=fbnf[:]).then_inc(s_fbf, 1)
            act.wait_ge(s_fbf, 1)
            copy(fbn[:], fbnf[:]).then_inc(s_fbn, 1)
            base_rows(2)
            turned_agg(0)
            turned_agg(1)
            base_rows(3)
            block0(1)
            for e in (0, 1):
                turned_own(e)
                finished(e)
            turned_agg(2)
            turned_own(2)
            finished(2)
            turned_own(3)
            finished(3)
            turned_own(4)
            turned_agg(4)
            finished(4)

        @block.tensor
        def _(pe):
            pe.wait_ge(s_h, 16)
            pe.wait_ge(s_diag, BITS + 1)
            pe.wait_ge(s_table, 1)
            pe.wait_ge(s_one, 1)

            def compact(f):
                ph, u = PHASES[f], B[f]
                pe.wait_ge(u.s_cls, 1)
                pe.matmul(before(ph), hc[:, H_TRI:H_TRI + P], u.cls[:], start=True, stop=False)
                for t in range(ph.tiles - 1):
                    last = pe.matmul(before(ph)[:, :, t + 1:], ones[:],
                                     u.cls[:, :, t:t + 1].to_broadcast([P, 4, ph.tiles - 1 - t]),
                                     start=False, stop=(t == ph.tiles - 2))
                last.then_inc(u.s_bef, 1)
                pe.wait_ge(u.s_rec, 1)
                if f:
                    pe.wait_ge(B[f - 1].s_R, 2)
                for t in range(ph.tiles):
                    pe.wait_ge(u.s_hot, t + 1)
                    for k in range(BLOCKS):
                        last = pe.matmul(recs[:, k, :], hot[:, t, k * P:(k + 1) * P],
                                         rec[:, ph.lo + t, :], start=(t == 0 and k == 0),
                                         stop=(t == ph.tiles - 1), skip_group_check=True)
                    last.then_inc(u.s_put, 1)

            def base_rows(g):
                if g == 0:
                    pe.wait_ge(s_x, 16)
                    pe.wait_ge(s_wti, 1)
                    pe.wait_ge(s_bp, 1)
                for k in range(4):
                    last = pe.transpose(ps_o[:, 1, k * P:(k + 1) * P], xs[:, 4 * g + k, :], ident[:])
                last.then_inc(s_bt, 1)
                if g:
                    pe.wait_ge(s_bc, g)
                for i in range(3):
                    pe.matmul(ps_o[:, 0, :], oneb[:], bparts[:, i].rearrange("p k d -> p (k d)"),
                              start=(i == 0), stop=False, skip_group_check=True)
                pe.wait_ge(s_btc, g + 1)
                for k in range(4):
                    last = pe.matmul(ps_o[:, 0, k * D:(k + 1) * D], xT[:, (4 * g + k) * P:(4 * g + k + 1) * P],
                                     wTi[:], start=False, stop=True, skip_group_check=True)
                last.then_inc(s_bo, 1)

            def block0(f):
                u = B[f]
                if f:
                    pe.wait_ge(B[0].s_lraw, 2)
                for j in range(SIDE):
                    pe.wait_ge(u.s_g[j], 16)
                    last = pe.transpose(ps_t[:, j // 4, (j % 4) * P:(j % 4 + 1) * P], u.G[:, j, :], ident[:])
                    if j in (3, SIDE - 1):
                        last.then_inc(u.s_lt, 1)

            def weights(f):
                u = B[f]
                pe.wait_ge(u.s_dw, 1)
                if f:
                    pe.wait_ge(B[0].s_aggL, 1)
                pe.matmul(lweight(), ones[0:LSLOTS, :], u.diagw[:],
                          start=True, stop=True).then_inc(u.s_lw, 1)

            def turn(e):
                f, k = ENDS[e]
                pe.wait_ge(B[f].s_agg[k - 1], 1)
                if e:
                    pe.wait_ge(s_ac, turn_of(e) - 1)
                pe.transpose(turned, B[f].agg[:, k - 1, :], ident[:]).then_inc(s_at, 1)

            def turn_own(e):
                pe.wait_ge(s_own[e], 16)
                if e:
                    pe.wait_ge(s_oc, e)
                pe.transpose(ps_o[:, 0, 0:P], own[:, e, :], ident[:]).then_inc(s_ot, 1)

            def own_part(e):
                if e >= len(finish):
                    pe.wait_ge(s_yc, e + 1 - len(finish))
                for i in range(3):
                    pe.matmul(finish[e % len(finish)], oneb[:], bparts[:, i, 0, :], start=(i == 0), stop=False)
                pe.wait_ge(s_oc, e + 1)
                pe.matmul(finish[e % len(finish)], ownT[:, e, :], wTi[:], start=False, stop=False)

            def agg_part(e):
                if e == LX:
                    pe.wait_ge(B[1].s_aggL, 1)
                else:
                    pe.wait_ge(s_ac, turn_of(e))
                pe.matmul(finish[e % len(finish)], aggT[:, e, :], wT[:], start=False, stop=True).then_inc(s_y, 1)

            for t in range(NT):
                mask_made(pe, t)
                if t >= 2:
                    pe.wait_ge(s_word, t - 1)
                for q in range(BITS):
                    pe.matmul(ps_code[:, t % 2, :], diags[:, q, :],
                              mask[:, t % MASKS, q * GROUPS:(q + 1) * GROUPS], start=(q == 0), stop=False)
                pe.matmul(ps_code[:, t % 2, :], hc[:, H_ID:H_ID + P], groups[:],
                          start=False, stop=True).then_inc(s_code, 1)
                if t == 1:
                    pe.wait_ge(s_w, 16)
                    pe.transpose(ps_t[:, 0, 0:D], wsb[:], ident[:]).then_inc(s_wt, 1)
                if t == PHASES[0].hi:
                    compact(0)
            compact(1)
            base_rows(0)
            block0(0)
            weights(0)
            base_rows(1)
            pe.wait_ge(s_fb, 2)
            pe.wait_ge(B[1].s_R, 2)
            pe.matmul(fbcount, ones[:], fb[:], start=True, stop=True).then_inc(s_fbc, 1)
            base_rows(2)
            pe.wait_ge(s_word, NT)
            turn(0)
            turn(1)
            base_rows(3)
            block0(1)
            pe.wait_ge(s_bc, 4)
            pe.wait_ge(s_fbn, 1)
            for e in (0, 1):
                turn_own(e)
                own_part(e)
                agg_part(e)
            weights(1)
            turn(2)
            turn_own(2)
            own_part(2)
            agg_part(2)
            turn_own(3)
            own_part(3)
            agg_part(3)
            turn_own(4)
            turn(4)
            own_part(4)
            agg_part(4)

            n = pe.value_load(fbn[0:1, 0:1], min_val=0, max_val=N)
            with pe.If(n > 0):
                pe.matmul(fbfront, hc[:, H_TRI:H_TRI + P], fb[:], start=True, stop=False)
                for t in range(NT - 1):
                    last = pe.matmul(fbfront[:, t + 1:NT], ones[:],
                                     fb[:, t:t + 1].to_broadcast([P, NT - 1 - t]), start=False, stop=(t == NT - 2))
                last.then_inc(s_fpre, 1)
                with pe.Fori(0, n) as i:
                    pe.wait_ge(s_fc, i + 1)
                    pe.matmul(fout, fcol[:], wT[:], start=True, stop=False)
                    pe.matmul(fout, fxcol[:], wTi[:], start=False, stop=False)
                    pe.matmul(fout, onerow[:, 0:1], brow[:], start=False, stop=True).then_inc(s_fp, 1)

        @block.vector
        def _(dve):
            V = nc.vector
            steps = [0]

            def step(instruction):
                steps[0] += 1
                return instruction.then_inc(s_v, 1)

            def settle(between=None):
                n = steps[0]
                if between:
                    between()
                dve.wait_ge(s_v, n)

            V.memset(onerow[:], 1.0)
            V.memset(oneb[:], 1.0)
            V.memset(ones[:], 1.0).then_inc(s_one, 1)

            def make_mask(t):
                dve.wait_ge(s_adj[t], 16)
                if t >= MASKS:
                    dve.wait_ge(s_code, t - MASKS + 1)
                    dve.wait_ge(s_cnt[(t - MASKS) in ACT_TILES], made(t - MASKS))
                V.tensor_scalar(mask[:, t % MASKS, :], A[:, t % RING, :], 0.0, None, ALU.not_equal).then_inc(s_mask, 1)

            def search(t, q):
                if q == 0:
                    dve.wait_ge(s_code, t + 1)
                last = V.max(codes[:, t, 8 * q:8 * q + 8], ps_code[:, t % 2, q * GQ:(q + 1) * GQ])
                if q == QUARTERS - 1:
                    last.then_inc(s_word, 1)

            def const(ph, at):
                return cc[:, at:at + 4].unsqueeze(2).to_broadcast([P, 4, ph.tiles])

            def classify(f):
                dve.wait_ge(s_c, 16)
                ph, u = PHASES[f], B[f]
                r = slice(ph.lo, ph.hi)
                wide = [P, 4, ph.tiles]
                dve.wait_ge(s_word, ph.hi)
                dve.wait_ge(s_cnt[0], made(ph.hi - 1) if ph.hi - 1 not in ACT_TILES else ph.hi - made(ph.hi - 1))
                if any(t in ACT_TILES for t in range(ph.hi)):
                    dve.wait_ge(s_cnt[1], sum(t in ACT_TILES for t in range(ph.hi)))
                n_row = cnt[:, r].unsqueeze(1).to_broadcast(wide)
                step(V.tensor_tensor(u.ge[:], n_row, const(ph, C_LEAST), ALU.is_ge))
                step(V.tensor_tensor(u.le[:], n_row, const(ph, C_MOST), ALU.is_le))
                eighth = codes[:, r].rearrange("p t (q e) -> p t q e", e=8)[:, :, :, 7]
                step(V.tensor_reduce(full[:, r], eighth, AX.X, ALU.max))
                settle()
                step(V.tensor_tensor(u.ge[:], u.ge[:], u.le[:], ALU.mult))
                step(V.tensor_scalar(ok[:, r], full[:, r], float(GROUPS), None, ALU.is_lt))
                settle()
                V.tensor_tensor(u.cls[:], u.ge[:], ok[:, r].unsqueeze(1).to_broadcast(wide), ALU.mult).then_inc(u.s_cls, 1)
                V.tensor_single_scalar(part[:, r, 0, :], codes[:, r], GROUPS - 1, ALU.bitwise_and)
                V.tensor_single_scalar(part[:, r, 1, :], codes[:, r], 9, ALU.logical_shift_right).then_inc(u.s_part, 1)

            def place(f):
                ph, u = PHASES[f], B[f]
                r = slice(ph.lo, ph.hi)
                dve.wait_ge(u.s_cls, 1)
                dve.wait_ge(u.s_bef, 1)
                step(V.tensor_tensor(u.le[:], before(ph), const(ph, C_CAP + 8 * f), ALU.is_lt))
                step(V.tensor_tensor(u.at[:], before(ph), const(ph, C_CAP + 8 * f + 4), ALU.add))
                settle()
                step(V.tensor_tensor(u.fits[:], u.le[:], u.cls[:], ALU.mult))
                settle()
                step(V.tensor_tensor(u.at[:], u.at[:], u.fits[:], ALU.mult))
                settle()
                step(V.tensor_reduce(slot[:, r], u.at[:].rearrange("p c t -> p t c"), AX.X, ALU.add))
                settle()
                dve.wait_ge(s_table, 3)
                if f:
                    dve.wait_ge(B[f - 1].s_put, PHASES[f - 1].tiles)
                for t in range(ph.tiles):
                    V.tensor_scalar(hot[:, t, :], slots[:],
                                    slot[:, ph.lo + t:ph.lo + t + 1], None, ALU.is_equal).then_inc(u.s_hot, 1)

            def count_placed(f):
                r = slice(PHASES[f].lo, PHASES[f].hi)
                step(V.tensor_reduce(placed[:, r], B[f].fits[:].rearrange("p c t -> p t c"), AX.X, ALU.add))

            def left_over(f):
                r = slice(PHASES[f].lo, PHASES[f].hi)
                V.scalar_tensor_tensor(fb[:, r], cnt[:, r], float(LEAST[0]), placed[:, r], ALU.is_ge,
                                       ALU.subtract).then_inc(s_fb, 1)

            def decode(u, blocks, between=None):
                dve.wait_ge(u.s_R, 1)
                for q in range(BITS):
                    step(V.tensor_scalar(u.bit[:, q, blocks], u.bits[:, blocks], q, 1,
                                         ALU.logical_shift_right, ALU.bitwise_and))
                settle(between)
                dve.wait_ge(u.s_R, 2)
                for q in range(BITS):
                    step(V.scalar_tensor_tensor(u.keys[:, blocks, q, :], u.R[:, blocks, 0:WORDS],
                                                float(1 + GROUPS * (BITS - 1 - q)), u.bit[:, q, blocks],
                                                ALU.add, ALU.mult))

            def neighbours_lx(f, between):
                gap = iter(between)
                u = B[f]
                decode(u, slice(0, 1), next(gap))
                n_slot = u.R[:, 0, 2 * WORDS + 2:2 * WORDS + 3]
                step(V.tensor_scalar(u.eq[:], cc[:, C_LO:C_LO + 4], n_slot, None, ALU.is_equal))
                step(V.tensor_scalar(u.lv[:], cc[:, C_V:C_V + 8], n_slot, None, ALU.is_le))
                settle(next(gap))
                V.scalar_tensor_tensor(u.em[:], cc[:, C_HI:C_HI + 4], n_slot, u.eq[:], ALU.is_equal,
                                       ALU.add).then_inc(u.s_em, 1)
                keys = u.keys[:, 0].rearrange("p b w -> p (b w)")
                step(V.max(u.top[:, 0, :], keys))
                settle(next(gap))
                dve.wait_ge(u.s_em, 1)
                step(V.match_replace(u.keyr[:], u.top[:, 0, :], keys, 0.0))
                settle(next(gap))
                step(V.max(u.top[:, 1, :], u.keyr[:]))
                settle(next(gap))
                tl = u.top[:, 0:2, :].rearrange("p a b -> p (a b)")
                h = LSLOTS
                step(V.tensor_scalar(u.lk[h:P, 0, :], tl[h:P, 5:13], u.em[h:P, 0:1], None, ALU.mult))
                step(V.tensor_tensor(u.lkv[0:h, :], tl[0:h, 0:8], u.lv[0:h, :], ALU.mult))
                for i in range(1, 4):
                    settle(next(gap))
                    step(V.scalar_tensor_tensor(u.lk[h:P, i, :], tl[h:P, 5 + i:13 + i], u.em[h:P, i:i + 1],
                                                u.lk[h:P, i - 1, :], ALU.mult, ALU.add))
                settle(next(gap))
                step(V.tensor_tensor(u.lkv[h:P, :], u.lk[h:P, 3, :], u.lv[h:P, :], ALU.mult))
                settle(next(gap))
                V.tensor_scalar(u.nbL[:], u.lkv[:], -1.0, float(N), ALU.mult, ALU.add).then_inc(u.s_nbL, 1)

            def neighbours_ms(f):
                u = B[f]
                decode(u, slice(1, BLOCKS))
                settle()
                for k in range(1, BLOCKS):
                    step(V.max(u.top[:, 1 + k, :], u.keys[:, k].rearrange("p b w -> p (b w)")))
                settle()
                V.tensor_scalar(u.nb[:], u.top[:, 2:, :], -1.0, float(N), ALU.mult, ALU.add).then_inc(u.s_nb, 1)

            def row_numbers(f):
                u = B[f]
                step(V.scalar_tensor_tensor(u.rid[:], u.R[:, :, 2 * WORDS], float(P), u.R[:, :, 2 * WORDS + 1],
                                            ALU.mult, ALU.add))
                step(V.tensor_scalar(u.none[:], u.R[:, :, 2 * WORDS + 2], 0.0, float(2 * N), ALU.is_equal, ALU.mult))

            def end_rows(f):
                u = B[f]
                side = slice(f * LSLOTS, (f + 1) * LSLOTS)
                V.tensor_tensor(endrow[side, LX:LX + 1], u.rid[side, 0:1], u.none[side, 0:1], ALU.add)
                ms = slice(2, 5, 2) if f else slice(0, 2)
                V.tensor_tensor(endrow[:, ms], u.rid[:, 1:], u.none[:, 1:],
                                ALU.add).then_inc(s_endrow, 1)

            def smallest(f, slots):
                raw = B[f].Lraw[:].rearrange("p j c r -> p r j c")
                dve.wait_ge(B[f].s_lraw, 2)
                for i in slots:
                    step(V.max(B[f].small[:, i, :], raw[:, i]))

            def largest(f):
                for i in range(LUSED - PHASES[f].lcap):
                    step(V.max(B[f].large[:, i, :], B[f].xpos[:, :, i]))

            def sum_two(f):
                u, lc = B[f], PHASES[f].lcap
                for i, (a, b, r) in enumerate(((1, 3, slice(0, lc)), (2, 4, slice(0, lc)),
                                               (2, 5, slice(lc, LUSED)), (3, 6, slice(lc, LUSED)))):
                    step(V.tensor_tensor(u.sumt[:, i % 2, r], u.small[:, r, a], u.small[:, r, b], ALU.add))

            def sum_three(f):
                u, n, lc = B[f], LUSED, PHASES[f].lcap
                for i, k in enumerate((5, 7)):
                    step(V.tensor_tensor(u.sums[:, i, 0:lc], u.sumt[:, i, 0:lc], u.small[:, 0:lc, k], ALU.add))
                for i, k in enumerate((8, 10)):
                    step(V.tensor_tensor(u.sums[:, i, lc:n], u.sumt[:, i, lc:n], u.large[:, :, 2 * SIDE - 1 - k],
                                         ALU.subtract))

            def weigh(f):
                u, n, lc = B[f], LUSED, PHASES[f].lcap
                dve.wait_ge(u.s_lw, 1)
                lw = lweight()
                step(V.tensor_tensor(u.sumt[:, :, 0:lc], lw[:, 0:2, 0:lc], u.sums[:, :, 0:lc], ALU.mult))
                step(V.tensor_tensor(u.sumt[:, :, lc:n], lw[:, 2:4, lc:n], u.sums[:, :, lc:n], ALU.mult))

            def aggregate(f):
                at = f * LSLOTS
                dve.wait_ge(s_fill, 1)
                V.scalar_tensor_tensor(aggT[:, LX, at:at + LUSED], B[f].sumt[:, 0, :], -1.0, B[f].sumt[:, 1, :],
                                       ALU.mult, ALU.subtract).then_inc(B[f].s_aggL, 1)

            def s_pairs(f):
                u = B[f]
                for g in range(G_S, NG):
                    dve.wait_ge(u.s_g[g], 16)
                a, b = u.G[:, G_S:NG:2, :], u.G[:, G_S + 1:NG:2, :]
                step(V.tensor_tensor(s4[:, 0:2], a, b, ALU.min))
                step(V.tensor_tensor(s4[:, 2:4], a, b, ALU.max))

            def s_inner():
                step(V.tensor_tensor(s4[:, 4], s4[:, 2], s4[:, 3], ALU.min))
                step(V.tensor_tensor(s4[:, 5], s4[:, 0], s4[:, 1], ALU.add))

            def s_sum(f):
                V.tensor_tensor(B[f].agg[:, 1], s4[:, 4], s4[:, 5], ALU.add).then_inc(B[f].s_agg[1], 1)

            def class_m(f, between):
                u = B[f]
                gap = iter(between)
                for g in range(G_M, G_S):
                    dve.wait_ge(u.s_g[g], 16)

                def two(i, j):
                    return scr[:, i:j + 1:j - i, :]

                a, b = u.G[:, G_M:G_M + 3, :], u.G[:, G_M + 3:G_S, :]
                step(V.tensor_tensor(scr[:, 0:3, :], a, b, ALU.min))
                step(V.tensor_tensor(scr[:, 6:9, :], a, b, ALU.max))
                settle(next(gap))
                step(V.tensor_tensor(two(3, 4), two(1, 7), two(2, 8), ALU.min))
                step(V.tensor_tensor(two(9, 10), two(1, 7), two(2, 8), ALU.max))
                settle(next(gap))
                step(V.tensor_tensor(two(1, 2), two(0, 9), two(4, 6), ALU.min))
                step(V.tensor_tensor(two(5, 7), two(0, 9), two(4, 6), ALU.max))
                settle(next(gap))
                step(V.tensor_tensor(two(0, 4), two(1, 2), two(3, 5), ALU.max))
                step(V.tensor_tensor(two(6, 8), two(2, 10), two(5, 7), ALU.min))
                settle(next(gap))
                step(V.tensor_tensor(scr[:, 9], scr[:, 4], scr[:, 8], ALU.max))
                step(V.tensor_tensor(scr[:, 11], scr[:, 0], scr[:, 6], ALU.add))
                settle(next(gap))
                V.tensor_tensor(u.agg[:, 0], scr[:, 9], scr[:, 11], ALU.add).then_inc(u.s_agg[0], 1)

            def mask_ahead(t):
                if t + 2 < NT and t + 2 not in ACT_TILES:
                    make_mask(t + 2)

            def tile(t):
                mask_ahead(t)
                for q in range(QUARTERS):
                    search(t, q)

            make_mask(0)
            make_mask(1)
            for t in range(PHASES[0].hi):
                tile(t)
                if t != 2:
                    continue
                dve.wait_ge(s_wc, 1)
                V.scalar_tensor_tensor(wTi[:], wT[:], 0.5, ident[:], ALU.mult, ALU.add).then_inc(s_wti, 1)
                dve.wait_ge(s_b, 16)
                for k in range(4):
                    step(V.tensor_copy(b4[:, k, :], brow[:]))
                settle()
                left = b4[:]
                for i in range(2):
                    step(V.tensor_copy(bparts[:, i], left))
                    settle()
                    step(V.tensor_tensor(bleft[:, i], left, bparts[:, i], ALU.subtract))
                    settle()
                    left = bleft[:, i]
                V.tensor_copy(bparts[:, 2], left).then_inc(s_bp, 1)
            t = PHASES[0].hi
            classify(0)
            for q in range(QUARTERS):
                search(t, q)
            place(0)
            mask_ahead(t)
            mask_ahead(t + 1)
            quarters = [lambda t=t + 1 + i // QUARTERS, q=i % QUARTERS: search(t, q) for i in range(2 * QUARTERS)]
            neighbours_ms(0)
            neighbours_lx(0, quarters + [lambda: row_numbers(0), None])
            end_rows(0)
            mask_ahead(t + 2)
            tile(t + 3)
            for t in range(t + 4, NT):
                tile(t)
            classify(1)
            place(1)
            count_placed(0)
            count_placed(1)
            settle()
            left_over(0)
            left_over(1)
            neighbours_ms(1)
            neighbours_lx(1, [
                lambda: row_numbers(1),
                None,
                lambda: end_rows(1),
                lambda: s_pairs(0),
                None,
                s_inner,
                None,
                lambda: s_sum(0),
                None, None])
            class_m(0, [lambda i=i: smallest(0, range(2 * i, 2 * i + 2)) for i in range(5)])
            smallest(0, range(10, LUSED))
            class_m(1, [
                lambda: largest(0),
                lambda: sum_two(0),
                None,
                lambda: sum_three(0),
                lambda: smallest(1, range(2))])
            weigh(0)
            settle(lambda: smallest(1, range(2, 4)))
            aggregate(0)
            smallest(1, range(4, LUSED))
            largest(1)
            settle()
            sum_two(1)
            settle()
            sum_three(1)
            settle()
            weigh(1)
            settle()
            aggregate(1)
            s_pairs(1)
            settle()
            s_inner()
            settle()
            s_sum(1)

            dve.wait_ge(s_fbn, 1)
            n = dve.value_load(fbn[0:1, 0:1], min_val=0, max_val=N)
            with dve.If(n > 0):
                is_nb, rnk = A[:, 1, :].bitcast(F32), A[:, 2, :].bitcast(F32)
                kept, vals, below = A[:, 3, :], A[:, 4, :].bitcast(F32), A[:, 5, :].bitcast(F32)
                all_ones = A[:, 6, :].bitcast(F32)
                V.memset(all_ones, 1.0)
                tp = hc[:, H_TP:].rearrange("p (t a) -> p t a", a=2)
                dve.wait_ge(s_fpre, 1)
                V.tensor_scalar(fbpos[:], fb[:], -2.0 * N, 2.0 * N, ALU.mult, ALU.add)
                dve.drain()
                V.tensor_tensor(fbat[:], fbpos[:], fbfront, ALU.add)
                V.scalar_tensor_tensor(fbrow[:], tp[:, :, 0], float(P), tp[:, :, 1], ALU.mult, ALU.add).then_inc(s_fat, 1)
                dve.wait_ge(s_list, 16 * NT)
                with dve.Fori(0, n) as i:
                    row = dve.value_load(rowlist[bass.ds(i, 1), :], min_val=0, max_val=N - 1)
                    V.tensor_copy(fxcol[:], xT[:, bass.ds(row, 1)])
                    V.memset(vals, BIG)
                    V.memset(fpre[:], 0)
                    V.memset(fbit[:], -2**31)
                    dve.wait_ge(s_fa, i * 16 + 16)
                    V.tensor_scalar(is_nb, A[:, 0, :], 0.0, None, ALU.not_equal)
                    dve.drain()
                    V.tensor_tensor_scan(rnk, all_ones, is_nb, 0.0, ALU.mult, ALU.add)
                    dve.drain()
                    V.tensor_scalar(fm[:, 1:2], rnk[:, N - 1:N], 0.5, 0.25, ALU.mult, ALU.add)
                    dve.drain()
                    V.tensor_scalar(fm[:, 0:1], fm[:, 1:2], MAGIC, -MAGIC, ALU.add, ALU.add)
                    dve.drain()
                    V.tensor_scalar(fm[:, 1:2], fm[:, 0:1], 2.0, None, ALU.mult)
                    V.scalar_tensor_tensor(is_nb, rnk, fm[:, 0:1], is_nb, ALU.not_equal, ALU.mult)
                    for j, q in enumerate((0.25, 0.5, 0.75)):
                        V.tensor_scalar(fk[:, j:j + 1], fm[:, 0:1], 2 * q, 0.375 - 2 * q, ALU.mult, ALU.add)
                    dve.drain()
                    V.scalar_tensor_tensor(kept, rnk, fm[:, 1:2], is_nb, ALU.not_equal, ALU.mult)
                    V.tensor_scalar(fcnt[:], fk[:], MAGIC, -MAGIC, ALU.add, ALU.add)
                    dve.drain()
                    V.copy_predicated(vals, kept, xT[:])
                    V.tensor_scalar(fk[:], fcnt[:], -1.0, None, ALU.add)
                    dve.drain()
                    with dve.Fori(0, 32):
                        V.tensor_tensor(fcand[:], fpre[:], fbit[:], ALU.bitwise_or)
                        dve.drain()
                        V.tensor_scalar(fsgn[:], fcand[:], 31, -1, ALU.arith_shift_right, ALU.bitwise_xor)
                        dve.drain()
                        V.scalar_tensor_tensor(fval[:], fsgn[:], -2**31, fcand[:], ALU.bitwise_or, ALU.bitwise_xor)
                        dve.drain()
                        for j in range(3):
                            V.tensor_scalar(below, vals, fval[:, j:j + 1].bitcast(F32), None, ALU.is_lt, ALU.add,
                                            accum_out=fcnt[:, j:j + 1])
                            dve.drain()
                        V.tensor_tensor(ftake[:], fcnt[:], fk[:], ALU.is_le)
                        dve.drain()
                        V.copy_predicated(fpre[:], ftake[:], fcand[:])
                        dve.drain()
                        V.tensor_single_scalar(fbit[:], fbit[:], 1, ALU.logical_shift_right)
                        dve.drain()
                    V.tensor_scalar(fsgn[:], fpre[:], 31, -1, ALU.arith_shift_right, ALU.bitwise_xor)
                    dve.drain()
                    V.scalar_tensor_tensor(fval[:], fsgn[:], -2**31, fpre[:], ALU.bitwise_or, ALU.bitwise_xor)
                    dve.drain()
                    V.tensor_scalar(fcnt[:], fval[:].bitcast(F32), THIRD / 2, None, ALU.mult)
                    dve.drain()
                    V.tensor_reduce(fcol[:], fcnt[:], AX.X, ALU.add).then_inc(s_fc, 1)
                    dve.wait_ge(s_fp, i + 1)
                    V.tensor_copy(frow[:], fout).then_inc(s_fy, 1)


def kernel(x, adj, L0_gnn_W, L0_gnn_b):
    import concourse.bacc as bacc
    from concourse.bass_utils import run_bass_kernel_spmd as run

    nc = bacc.Bacc("TRN2", target_bir_lowering=False, num_devices=1)
    hconst, cconst = constants()
    arrays = {
        "x_dram": np.ascontiguousarray(x),
        "adj_dram": np.ascontiguousarray(adj),
        "w_dram": np.ascontiguousarray(L0_gnn_W),
        "b_dram": np.ascontiguousarray(L0_gnn_b).reshape(1, D),
        "hconst_dram": hconst,
        "cconst_dram": cconst,
    }
    args = [nc.dram_tensor(k, a.shape, mybir.dt.from_np(a.dtype), kind="ExternalInput").ap()
            for k, a in arrays.items()]
    out = nc.dram_tensor("out_dram", (N, D), F32, kind="ExternalOutput").ap()
    build(nc, *args, out)
    return run(nc, [arrays], core_ids=[0]).results[0]["out_dram"]
```
